# Optimizing a Trainium2 kernel written in Bass

```python
import numpy as np
import jax
import jax.numpy as jnp

def _softmax(x, axis=-1):
    return jax.nn.softmax(x, axis=axis)

def _gelu(x):
    return jax.nn.gelu(x, approximate=True)

def _silu(x):
    return jax.nn.silu(x)

def _sigmoid(x):
    return jax.nn.sigmoid(x)

def _layernorm(x, axis=-1, eps=1e-05):
    m = jnp.mean(x, axis=axis, keepdims=True)
    v = jnp.var(x, axis=axis, keepdims=True)
    return (x - m) / jnp.sqrt(v + eps)

def _scatter_add(tgt, idx, src, axis=0):
    return tgt.at[idx].add(src)

def _segment_sum(src, seg, n):
    return jax.ops.segment_sum(src, seg, n)
kernel_name = 'mk_early_fusion_d1_tok_img512_r4_8a9793'

def setup_inputs(seed: int=0):
    np.random.seed(seed)
    _w = jnp.asarray

    def _rec_inputs():
        import jax
        import jax.numpy as jnp
        _rk = jax.random.key(seed)
        x = -0.000147625 + 0.999875 * jax.random.normal(jax.random.fold_in(_rk, 1), (4, 3, 224, 224), jnp.float32)
        txt = 0.00355565 + 0.408319 * jax.random.normal(jax.random.fold_in(_rk, 2), (4, 512, 128), jnp.float32)
        return (x, txt)
    x, txt = _rec_inputs()

    def _L0_tok_setup():
        import jax, jax.numpy as jnp
        import numpy as np
        N_PATCHES = 8
        PATCH = 28
        C = 3
        IN_D = C * PATCH * PATCH
        HID = 128
        SEQ = N_PATCHES * N_PATCHES + 1

        def _positional_embedding(seq_len, dim):
            i = np.arange(seq_len)[:, None].astype(np.float32)
            j = np.arange(dim)[None, :].astype(np.float32)
            ang = i / np.power(100000.0, j / dim)
            pe = np.where(j % 2 == 0, np.sin(ang), np.cos(ang))
            return jnp.asarray(pe, dtype=jnp.float32)
        key = jax.random.key(seed)
        k1, k2, k3, k4 = jax.random.split(key, 4)
        B = 64
        X = jax.random.normal(k1, (B, C, 224, 224), dtype=jnp.float32)
        bound = 1.0 / np.sqrt(IN_D)
        W = jax.random.uniform(k2, (HID, IN_D), minval=-bound, maxval=bound, dtype=jnp.float32)
        b = jax.random.uniform(k3, (HID,), minval=-bound, maxval=bound, dtype=jnp.float32)
        class_token = jax.random.uniform(k4, (1, HID), dtype=jnp.float32)
        pos_embed = _positional_embedding(SEQ, HID)
        return {'X': X, 'W': W, 'b': b, 'class_token': class_token, 'pos_embed': pos_embed}
    _L0_tok_all = _L0_tok_setup()
    _L0_tok_in = {k: v for k, v in _L0_tok_all.items() if k in ('W', 'b', 'class_token', 'pos_embed')}
    del _L0_tok_all

    def _L0_attn_setup():
        import jax, jax.numpy as jnp
        import numpy as np
        B, S, D = (8, 256, 128)
        K, H = (64, 8)
        key = jax.random.key(seed)
        ks = jax.random.split(key, 8)
        s = lambda fan_in: 1.0 / np.sqrt(fan_in)
        return {'x': jax.random.normal(ks[0], (B, S, D), dtype=jnp.float32), 'Wq': jax.random.uniform(ks[1], (D, K * H), jnp.float32, -s(D), s(D)), 'Wk': jax.random.uniform(ks[2], (D, K * H), jnp.float32, -s(D), s(D)), 'Wv': jax.random.uniform(ks[3], (D, D * H), jnp.float32, -s(D), s(D)), 'Wo': jax.random.uniform(ks[4], (D * H, D), jnp.float32, -s(D * H), s(D * H)), 'bo': jax.random.uniform(ks[5], (D,), jnp.float32, -s(D * H), s(D * H)), 'gamma': jnp.ones((D,), jnp.float32), 'beta': jnp.zeros((D,), jnp.float32)}
    _L0_attn_all = _L0_attn_setup()
    _L0_attn_in = {k: v for k, v in _L0_attn_all.items() if k in ('Wq', 'Wk', 'Wv', 'Wo', 'bo', 'gamma', 'beta')}
    del _L0_attn_all

    def _L0_ffn_setup():
        import jax, jax.numpy as jnp
        import numpy as np
        B, S, D, F, E = (4, 512, 128, 512, 8)
        key = jax.random.key(seed)
        k = jax.random.split(key, 5)
        x = jax.random.normal(k[0], (B, S, D), dtype=jnp.float32)
        Ws = jax.random.normal(k[1], (D, E), dtype=jnp.float32) * 0.02
        bs = jnp.zeros((E,), dtype=jnp.float32)
        W1 = jax.random.normal(k[2], (E, D, F), dtype=jnp.float32) * 0.02
        b1 = jnp.zeros((E, F), dtype=jnp.float32)
        W2 = jax.random.normal(k[3], (E, F, D), dtype=jnp.float32) * 0.02
        b2 = jnp.zeros((E, D), dtype=jnp.float32)
        return {'x': x, 'Ws': Ws, 'bs': bs, 'W1': W1, 'b1': b1, 'W2': W2, 'b2': b2}
    _L0_ffn_all = _L0_ffn_setup()
    _L0_ffn_in = {k: v for k, v in _L0_ffn_all.items() if k in ('Ws', 'bs', 'W1', 'b1', 'W2', 'b2')}
    del _L0_ffn_all
    return {'x': x, 'txt': txt, 'L0_tok_W': _L0_tok_in['W'], 'L0_tok_b': _L0_tok_in['b'], 'L0_tok_class_token': _L0_tok_in['class_token'], 'L0_tok_pos_embed': _L0_tok_in['pos_embed'], 'L0_attn_Wq': _L0_attn_in['Wq'], 'L0_attn_Wk': _L0_attn_in['Wk'], 'L0_attn_Wv': _L0_attn_in['Wv'], 'L0_attn_Wo': _L0_attn_in['Wo'], 'L0_attn_bo': _L0_attn_in['bo'], 'L0_attn_gamma': _L0_attn_in['gamma'], 'L0_attn_beta': _L0_attn_in['beta'], 'L0_ffn_Ws': _L0_ffn_in['Ws'], 'L0_ffn_bs': _L0_ffn_in['bs'], 'L0_ffn_W1': _L0_ffn_in['W1'], 'L0_ffn_b1': _L0_ffn_in['b1'], 'L0_ffn_W2': _L0_ffn_in['W2'], 'L0_ffn_b2': _L0_ffn_in['b2']}

def reference(x, txt, L0_tok_W, L0_tok_b, L0_tok_class_token, L0_tok_pos_embed, L0_attn_Wq, L0_attn_Wk, L0_attn_Wv, L0_attn_Wo, L0_attn_bo, L0_attn_gamma, L0_attn_beta, L0_ffn_Ws, L0_ffn_bs, L0_ffn_W1, L0_ffn_b1, L0_ffn_W2, L0_ffn_b2):
    import jax
    import jax.numpy as jnp

    def _L0_tok_ref(X, W, b, class_token, pos_embed):
        import jax, jax.numpy as jnp
        import numpy as np
        N_PATCHES = 8
        PATCH = 28
        C = 3
        IN_D = C * PATCH * PATCH
        HID = 128
        SEQ = N_PATCHES * N_PATCHES + 1

        def _positional_embedding(seq_len, dim):
            i = np.arange(seq_len)[:, None].astype(np.float32)
            j = np.arange(dim)[None, :].astype(np.float32)
            ang = i / np.power(100000.0, j / dim)
            pe = np.where(j % 2 == 0, np.sin(ang), np.cos(ang))
            return jnp.asarray(pe, dtype=jnp.float32)
        B = X.shape[0]
        patches = X.reshape(B, C, N_PATCHES, PATCH, N_PATCHES, PATCH)
        patches = patches.transpose(0, 2, 4, 1, 3, 5).reshape(B, N_PATCHES * N_PATCHES, IN_D)
        tokens = jnp.einsum('bpi,hi->bph', patches, W) + b
        cls = jnp.broadcast_to(class_token[None, :, :], (B, 1, HID))
        tokens = jnp.concatenate([cls, tokens], axis=1)
        return tokens * pos_embed[None, :, :]

    def _L0_attn_ref(x, Wq, Wk, Wv, Wo, bo, gamma, beta):
        import jax, jax.numpy as jnp
        import numpy as np
        B, S, D = (8, 256, 128)
        K, H = (64, 8)
        b, s, d = x.shape
        q = (x @ Wq).reshape(b, s, H, K)
        k = (x @ Wk).reshape(b, s, H, K)
        v = (x @ Wv).reshape(b, s, H, D)
        scores = jnp.einsum('bqhk,bshk->hbqs', q, k) / np.sqrt(K).astype(np.float32)
        scores = jnp.where(scores == 0, jnp.float32(-1000000000.0), scores)
        att = jax.nn.softmax(scores, axis=-1)
        o = jnp.einsum('hbqs,bshd->bqhd', att, v).reshape(b, s, H * D)
        o = o @ Wo + bo
        y = o + x
        mu = jnp.mean(y, axis=-1, keepdims=True)
        var = jnp.mean(jnp.square(y - mu), axis=-1, keepdims=True)
        return (y - mu) * jax.lax.rsqrt(var + 1e-06) * gamma + beta

    def _L0_ffn_ref(x, Ws, bs, W1, b1, W2, b2):
        import jax, jax.numpy as jnp
        import numpy as np
        B, S, D, F, E = (4, 512, 128, 512, 8)
        Bb, Ss, Dd = x.shape
        xt = x.reshape(-1, Dd)
        logits = xt @ Ws + bs
        probs = jax.nn.softmax(logits, axis=-1)
        prob_max = jnp.max(probs, axis=-1)
        routes = jnp.argmax(probs, axis=-1)
        onehot = jax.nn.one_hot(routes, W1.shape[0], dtype=xt.dtype)

        def expert_ffn(w1, bb1, w2, bb2):
            h = jax.nn.gelu(xt @ w1 + bb1, approximate=False)
            return h @ w2 + bb2
        y = jax.vmap(expert_ffn)(W1, b1, W2, b2)
        out = jnp.einsum('te,etd->td', onehot, y)
        out = out * prob_max[:, None]
        return out.reshape(Bb, Ss, Dd)
    h = _L0_tok_ref(x, L0_tok_W, L0_tok_b, L0_tok_class_token, L0_tok_pos_embed)
    h = jnp.concatenate([h, txt], axis=1)
    h = h + _L0_attn_ref(_layernorm(h, axis=-1), L0_attn_Wq, L0_attn_Wk, L0_attn_Wv, L0_attn_Wo, L0_attn_bo, L0_attn_gamma, L0_attn_beta)
    h = h + _L0_ffn_ref(_layernorm(h, axis=-1), L0_ffn_Ws, L0_ffn_bs, L0_ffn_W1, L0_ffn_b1, L0_ffn_W2, L0_ffn_b2)
    return h

_drawn_inputs = setup_inputs


def setup_inputs(seed=0):
    import zlib

    import numpy as np

    out = dict(_drawn_inputs(seed))
    spreads = {'L0_attn_gamma': (1.0, 0.2),
     'L0_attn_beta': (0.0, 0.1),
     'L0_ffn_bs': (0.0, 0.8),
     'L0_ffn_b1': (0.0, 0.8),
     'L0_ffn_b2': (0.0, 0.69)}
    factors = {'L0_tok_b': 8.0,
     'L0_attn_Wq': 7.092,
     'L0_attn_Wk': 7.02,
     'L0_attn_Wv': 4.698,
     'L0_attn_Wo': 4.445,
     'L0_attn_bo': 3.814,
     'L0_ffn_Ws': 4.476,
     'L0_ffn_W1': 8.0,
     'L0_ffn_W2': 8.0}
    for name, (base, spread) in spreads.items():
        noise = np.random.default_rng([zlib.crc32(name.encode()), seed]).standard_normal(out[name].shape)
        drawn = base * np.exp(spread * noise) if base else spread * noise
        out[name] = jnp.asarray(drawn.astype(out[name].dtype))
    for name, factor in factors.items():
        out[name] = (out[name] * factor).astype(out[name].dtype)
    return out
```

```python
from contextlib import ExitStack

import concourse.bass as bass
from concourse import mybir

F32 = mybir.dt.float32
F32R = mybir.dt.float32r
I32 = mybir.dt.int32
U32 = mybir.dt.uint32
ALU = mybir.AluOpType
ACT = mybir.ActivationFunctionType
AX = mybir.AxisListType

P = 128


def early_fusion_kernel(
    nc, x, txt, tok_W, tok_b, cls_tok, pos, Wq, Wk, Wv, Wo, bo, gamma, beta, Ws, bs, W1, b1, W2, b2, out, by_expert,
):
    B, C, IMG, _ = x.shape
    D = txt.shape[2]
    NTXT = txt.shape[1]
    SEQ = pos.shape[0]
    NPATCH = SEQ - 1
    GRID = int(round(NPATCH ** 0.5))
    PX = IMG // GRID
    CI = C * PX
    S = SEQ + NTXT
    K = 64
    H = Wq.shape[1] // K
    NX = NTXT // P
    NT = NX + 1
    TILES = B * NT
    SP = S + 1
    TAIL = SEQ
    E = Ws.shape[1]
    FF = W1.shape[2]
    NF = FF // P
    TOKENS = B * S
    SORTED = (TOKENS - E) // P + E
    ROW = 2 * D + 4
    SKIP = 1 << 20
    UN = 5
    assert D == P and NX * P == NTXT and SORTED % UN == 0 and SEQ <= P and H * K == 4 * P

    STEPS = NT * H
    FILLS = H + NT + STEPS
    FIRST_V, FIRST_S = H, H + NT
    PER_SLOT = [(FILLS + 1) // 2, FILLS // 2]

    with ExitStack() as ctx:
        def sb(name, shape, dt=F32):
            return ctx.enter_context(nc.sbuf_tensor(name, shape, dt))

        def psum(name, shape):
            return ctx.enter_context(nc.psum_tensor(name, shape, F32))

        def sem(name):
            return ctx.enter_context(nc.semaphore(name))

        ident = sb("ident", [P, P])
        ones = sb("ones", [P, P])
        before = sb("before", [P, P])
        h_all = sb("h_all", [P, TILES, D])
        y_all = sb("y_all", [P, TILES, D])
        xn_all = sb("xn_all", [P, TILES, D])
        xT_all = sb("xT_all", [P, B, NT * P])
        xs = sb("xs", [P, NT * P])
        WqS = sb("WqS", [P, H * K])
        WkS = sb("WkS", [P, H, 2, K])
        VO = sb("VO", [P, H * D])
        KH = sb("KH", [P, H, SP], F32R)
        KL = sb("KL", [P, H, SP], F32R)
        QS = sb("QS", [P, 2, H, P], F32R)
        V = sb("V", [P, TILES * ROW])
        Vt = V[:, 0:NT * H * D].rearrange("p (t n) -> p t n", t=NT)
        rows = V[:, :].rearrange("p (t c) -> p t c", c=ROW)
        WvT = V[:, 0:H * D]
        WvS = V[:, H * D:2 * H * D]
        WoS = V[:, 2 * H * D:3 * H * D].rearrange("p (h d) -> p h d", h=H)
        zero_mark = sb("zero_mark", [P, S])
        sneg = sb("sneg", [P, 2, S])
        rmax = sb("rmax", [P, 2])
        prob = sb("prob", [P, 2, S])
        den = sb("den", [P, 2])
        rden = sb("rden", [P, 2])
        pn = sb("pn", [P, 2, NT * P])
        pT = sb("pT", [P, 2, NT * P])
        stage = sb("stage", [P, max(B * GRID * IMG + C * PX * PX + PX * D, 3 * E * FF)])
        X = stage[0:CI, 0:B * GRID * IMG].rearrange("p (g w) -> p g w", w=IMG)
        at = B * GRID * IMG
        WtS = stage[:, at:at + C * PX * PX]
        at += C * PX * PX
        WtT = stage[0:CI, at:at + PX * D].rearrange("p (j d) -> p j d", d=D)
        W1S = stage[:, 0:E * FF]
        W2S = stage[:, E * FF:2 * E * FF]
        b1S = stage[:, 2 * E * FF:3 * E * FF]
        b2S = sb("b2S", [P, E * D])
        tokT = sb("tokT", [P, B * NPATCH])
        posS = sb("posS", [P, D])
        clsS = sb("clsS", [P, D])
        boS = sb("boS", [P, D])
        gammaS = sb("gammaS", [P, D])
        betaS = sb("betaS", [P, D])
        tbS = sb("tbS", [P, 1])
        WsS = sb("WsS", [P, E])
        bsS = sb("bsS", [P, E])
        mean = sb("mean", [P, TILES])
        var = sb("var", [P, TILES])
        rstd = sb("rstd", [P, TILES])
        half = sb("half", [P, TILES])
        tokid = sb("tokid", [P, TILES], I32)
        spare = prob[:, :, :].rearrange("p a n -> p (a n)")
        RT = E * TILES
        logit, psel = (spare[:, n * RT:(n + 1) * RT].rearrange("p (t e) -> p t e", e=E) for n in range(2))
        fresh, incl, base = (spare[:, n * RT:(n + 1) * RT].rearrange("p (e t) -> p e t", e=E) for n in range(2, 5))
        cmp = spare[:, 5 * RT:5 * RT + SORTED * E]
        lmax = sb("lmax", [P, TILES])
        psum_ = sb("psum_", [P, TILES])
        pbest = sb("pbest", [P, TILES])
        hot = sb("hot", [P, E, TILES])
        order = sb("order", [P, E])
        ramp = sb("ramp", [P, 32])
        rampi = sb("rampi", [P, 32], I32)
        rampP = sb("rampP", [P, 32])
        ntile = sb("ntile", [P, E])
        tend = sb("tend", [P, E])
        one8 = sb("one8", [P, E])
        valid = sb("valid", [P, TILES])
        slotf = sb("slotf", [P, TILES])
        slotu = sb("slotu", [P, TILES], U32)
        exf = sb("exf", [P, SORTED])
        exi = sb("exi", [P, SORTED], I32)
        blank = sb("blank", [P, ROW])
        ring = y_all[:, :, :].rearrange("p t d -> p (t d)")[:, 0:UN * ROW].rearrange("p (s c) -> p s c", c=ROW)
        fT = xn_all[:, 0:2, :]
        hid = xn_all[:, 4:12, :].rearrange("p (s a) d -> p s (a d)", s=2)
        hidT = xn_all[:, 12:20, :].rearrange("p (s a) d -> p s (a d)", s=2)
        act_h = xT_all[:, 0:2, 0:FF]
        yo = xT_all[:, 2:4, :].rearrange("p b (t d) -> p (b t) d", d=D)

        SL = psum("SL", [P, 4, 512])
        PT = psum("PT", [P, 2, 512])
        O = psum("O", [P, 512])
        Q = psum("Q", [P, 512])
        slots = [SL[:, 2 * s:2 * s + 2, :].rearrange("p a n -> p (a n)") for s in range(2)]
        PTf = PT[:, :, :].rearrange("p a n -> p (a n)")

        ld_txt, ld_attn, ld_small, ld_tok, ld_experts, ld_blank = (
            sem(n) for n in ("ld_txt", "ld_attn", "ld_small", "ld_tok", "ld_experts", "ld_blank"))
        consts_ready = sem("consts_ready")
        settled_vec, settled_pool = sem("settled_vec"), sem("settled_pool")
        pool_step = sem("pool_step")
        vec_step = sem("vec_step")
        act_step = sem("act_step")
        patches_in_h = sem("patches_in_h")
        stat_ready = sem("stat_ready")
        rstd_ready = sem("rstd_ready")
        centred = sem("centred")
        squared = sem("squared")
        normed = sem("normed")
        pre_fill = sem("pre_fill")
        pre_evac = sem("pre_evac")
        y_init = sem("y_init")
        xs_ready = sem("xs_ready")
        filled = sem("filled")
        free = [sem("free0"), sem("free1")]
        kh_done = sem("kh_done")
        q_psum = sem("q_psum")
        q_hi = sem("q_hi")
        q_lo = sem("q_lo")
        z_done = sem("z_done")
        exp_done = sem("exp_done")
        rden_done = sem("rden_done")
        p_normed = sem("p_normed")
        p_turned = sem("p_turned")
        pt_evac = sem("pt_evac")
        pv_done = sem("pv_done")
        y_done = sem("y_done")
        r_fill = sem("r_fill")
        r_evac = sem("r_evac")
        logits_done = sem("logits_done")
        l_ready = sem("l_ready")
        l_exp = sem("l_exp")
        hot_ready = sem("hot_ready")
        ranks_done = sem("ranks_done")
        slots_ready = sem("slots_ready")
        experts_ready = sem("experts_ready")
        rows_out = sem("rows_out")
        row_in = [sem(f"row_in{s}") for s in range(UN)]
        f_turned = sem("f_turned")
        fT_ready = sem("fT_ready")
        up_done = sem("up_done")
        up_biased = sem("up_biased")
        gelu_done = sem("gelu_done")
        hid_turned = sem("hid_turned")
        hidT_ready = sem("hidT_ready")
        down_done = sem("down_done")
        yb_done = sem("yb_done")
        yw_done = sem("yw_done")
        yo_ready = sem("yo_ready")
        out_done = [sem(f"out_done{s}") for s in range(UN)]

        out_rows = out.rearrange("b s d -> (b s) d")
        block = ctx.enter_context(nc.Block())

        @block.sync
        def _(sp):
            for b in range(B):
                sp.dma_start(h_all[:, b * NT:b * NT + NX, :],
                             txt[b].rearrange("(t p) d -> p t d", p=P)).then_inc(ld_txt, 16)
            sp.dma_start(WtS, tok_W[:, :]).then_inc(ld_tok, 16)
            for b in range(B):
                for c in range(C):
                    sp.dma_start(X[c * PX:(c + 1) * PX, b * GRID:(b + 1) * GRID, :],
                                 x[b, c].rearrange("(g i) w -> i g w", i=PX)).then_inc(ld_tok, 16)
            sp.wait_ge(pre_fill, 7)
            sp.dma_start(W1S.rearrange("p (e f) -> p e f", e=E), W1.rearrange("e d f -> d e f")).then_inc(ld_experts, 16)
            sp.dma_start(W2S.rearrange("p (e n d) -> p e n d", e=E, n=NF),
                         W2.rearrange("e (n p) d -> p e n d", p=P)).then_inc(ld_experts, 16)
            sp.dma_start(b1S, b1.rearrange("e f -> (e f)").partition_broadcast(P)).then_inc(ld_experts, 16)
            sp.wait_ge(consts_ready, 2)
            sp.dma_start(by_expert.rearrange("(t p) c -> p t c", p=P),
                         blank[:, :].unsqueeze(1).to_broadcast([P, SORTED, ROW])).then_inc(ld_blank, 16)
            sp.wait_ge(rows_out, 16 * TILES)
            for s in range(UN):
                sp.dma_start(ring[:, s, :], by_expert[s * P:(s + 1) * P, :]).then_inc(row_in[s], 16)
            with sp.Fori(1, SORTED // UN) as u:
                for s in range(UN):
                    if s == 0:
                        last_out, first_row = sp.snap(u * 16), sp.snap(u * (UN * P))
                    sp.wait_ge(out_done[s], last_out)
                    sp.dma_start(ring[:, s, :], by_expert[bass.ds(first_row + s * P, P), :]).then_inc(row_in[s], 16)

        @block.scalar
        def _(act):
            act.sem_inc(up_done)
            act.sem_inc(hid_turned)
            act.dma_start(WvS[:, :], Wv).then_inc(ld_attn, 16)
            act.dma_start(WoS[:, :, :], Wo.rearrange("(h v) d -> v h d", v=D)).then_inc(ld_attn, 16)
            act.dma_start(posS[0:NPATCH, :], pos[1:SEQ, :]).then_inc(ld_small, 16)
            act.dma_start(posS[NPATCH:SEQ, :], pos[0:1, :]).then_inc(ld_small, 16)
            act.dma_start(clsS[NPATCH:SEQ, :], cls_tok).then_inc(ld_small, 16)
            act.dma_start(tbS[:, :], tok_b.unsqueeze(1)).then_inc(ld_small, 16)
            for t, v in ((boS, bo), (gammaS, gamma), (betaS, beta), (bsS, bs)):
                act.dma_start(t[:, :], v.partition_broadcast(P)).then_inc(ld_small, 16)
            act.dma_start(WsS[:, :], Ws).then_inc(ld_small, 16)
            act.dma_start(b2S[:, :], b2.rearrange("e d -> (e d)").partition_broadcast(P)).then_inc(ld_small, 16)
            act.dma_start(WqS[:, :], Wq).then_inc(ld_attn, 16)
            for two in range(2):
                act.dma_start(WkS[:, :, two, :], Wk.rearrange("d (h k) -> d h k", h=H)).then_inc(ld_attn, 16)

            def squares(n, src, dst):
                act.wait_ge(centred, n)
                nc.scalar.activation(dst, src, ACT.Square).then_inc(squared, 1)

            act.wait_ge(pre_fill, 1)
            nc.scalar.activation(WvT, slots[0], ACT.Copy).then_inc(pre_evac, 1)
            act.wait_ge(pre_fill, 2)
            nc.scalar.activation(VO[:, :], slots[1], ACT.Copy).then_inc(pre_evac, 1)
            sq_all = xT_all[:, :, :].rearrange("p b (t d) -> p b t d", t=NT)
            xn_v = xn_all[:, :, :].rearrange("p (b t) d -> p b t d", t=NT)
            squares(1, xn_v[:, :, 0:NX, :], sq_all[:, :, 0:NX, :])
            for g in range(4):
                n = min(8, PX - 8 * g)
                act.wait_ge(pre_fill, 3 + g)
                nc.scalar.activation(WtT[:, 8 * g:8 * g + n, :].rearrange("p j d -> p (j d)"),
                                     slots[g % 2][0:CI, 0:n * D], ACT.Copy).then_inc(pre_evac, 1)
            act.wait_ge(pre_fill, 7)
            act.wait_ge(ld_small, 160)
            nc.scalar.activation(tokT[:, :], Q[:, 0:B * NPATCH], ACT.Identity, bias=tbS[:, 0:1]).then_inc(pre_evac, 1)
            squares(2, xn_v[:, :, NX, :], sq_all[:, :, NX, :])
            for b in range(B):
                act.wait_ge(pre_fill, 9 + b)
                nc.scalar.activation(xT_all[:, b, :], slots[b % 2][:, 0:NT * P], ACT.Copy).then_inc(pre_evac, 1)

            with act.Fori(0, B) as b:
                at_fill = act.snap(b * FILLS)
                at_step = act.snap(b * STEPS)
                at_tile = act.snap(b * NT)
                at_slot = [act.snap(b * PER_SLOT[0]), act.snap(b * PER_SLOT[1])]
                for h in range(H):
                    act.wait_ge(filled, at_fill + (h + 1))
                    nc.scalar.activation(KH[:, h, :], slots[h % 2][:, 0:SP], ACT.Copy).then_inc(kh_done, 1)
                for t in range(0, NT, 2):
                    n = FIRST_V + t
                    act.wait_ge(filled, at_fill + (n + 1))
                    nc.scalar.activation(Vt[:, t, :], slots[n % 2], ACT.Copy).then_inc(free[n % 2], 1)

                def queries(t):
                    act.wait_ge(q_psum, at_tile + (t + 2))
                    for par in range(2):
                        nc.scalar.activation(QS[0:K, t % 2, par::2, :],
                                             Q[K * par:K * par + K, :].rearrange("p (i m) -> p i m", m=P),
                                             ACT.Copy).then_inc(q_hi, 1)

                queries(0)

                def evacuate(g):
                    act.wait_ge(p_turned, at_step + (g + 1))
                    if g >= 2:
                        act.wait_ge(pv_done, at_step + (g - 1))
                    nc.scalar.activation(pT[:, g % 2, :], PTf[:, 0:NT * P], ACT.Copy).then_inc(pt_evac, 1)

                def exponentials(g):
                    n = FIRST_S + g
                    act.wait_ge(free[n % 2], at_slot[n % 2] + (n // 2 + 2))
                    if g >= 2:
                        act.wait_ge(p_normed, at_step + (g - 1))
                        act.wait_ge(rden_done, at_step + (g - 1))
                    nc.scalar.activation(prob[:, g % 2, :], sneg[:, g % 2, :], ACT.Exp, bias=rmax[:, g % 2:g % 2 + 1],
                                         scale=-1.0, accum_out=den[:, g % 2:g % 2 + 1]).then_inc(exp_done, 1)

                for g in range(STEPS):
                    exponentials(g)
                    if g % H == QSTEP and g // H + 1 < NT:
                        queries(g // H + 1)
                    if g >= 1:
                        evacuate(g - 1)
                evacuate(STEPS - 1)

            squares(3, xn_all[:, :, :], xT_all[:, :, :].rearrange("p b n -> p (b n)"))
            squares(4, rows[:, :, D:2 * D], xn_all[:, :, :])
            for q in range(NT):
                act.wait_ge(r_fill, q + 1)
                nc.scalar.activation(xT_all[:, :, :].rearrange("p b n -> p (b n)")[:, q * 512:(q + 1) * 512],
                                     SL[:, q % 2, :], ACT.Copy).then_inc(r_evac, 1)
            act.wait_ge(l_ready, 1)
            nc.scalar.activation(psel[:, :, :], psel[:, :, :], ACT.Exp).then_inc(l_exp, 1)

            with act.Fori(0, SORTED // UN) as u:
                at_u = act.snap(u * UN)
                for s in range(UN):
                    act.wait_ge(f_turned, at_u + (s + 1))
                    act.wait_ge(up_done, at_u + (max(s - 1, 0) + 1))
                    nc.scalar.activation(fT[:, s % 2, :], Q[:, 0:P], ACT.Copy).then_inc(fT_ready, 1)
                    act.wait_ge(up_biased, at_u + (s + 2))
                    act.wait_ge(hid_turned, at_u + (max(s - 1, 0) + 1))
                    nc.scalar.activation(act_h[:, s % 2, :], hid[:, s % 2, :], ACT.Gelu).then_inc(gelu_done, 1)

        @block.gpsimd
        def _(pool):
            pool.sem_inc(q_psum)
            n_step = [0]

            def settle_pool():
                pool.sem_inc(settled_pool)


            def step(ins):
                n_step[0] += 1
                ins.then_inc(pool_step, 1)
                pool.wait_ge(pool_step, n_step[0])

            step(nc.gpsimd.memset(ident[:, :], 0.0))
            step(nc.gpsimd.affine_select(out=ident[:, :], in_=ident[:, :], compare_op=ALU.not_equal, fill=1.0, base=0,
                                         pattern=[[-1, P]], channel_multiplier=1))
            nc.gpsimd.memset(half[:, :], -0.5).then_inc(consts_ready, 1)
            step(nc.gpsimd.memset(blank[:, :], 0.0))
            nc.gpsimd.memset(blank[:, 2 * D + 1:2 * D + 2].bitcast(I32), SKIP).then_inc(consts_ready, 1)
            step(nc.gpsimd.memset(ones[:, :], 1.0))
            step(nc.gpsimd.affine_select(out=before[:, :], in_=ones[:, :], compare_op=ALU.is_gt, fill=0.0, base=0,
                                         pattern=[[1, P]], channel_multiplier=-1))
            step(nc.gpsimd.iota(rampi[:, :], pattern=[[1, 32]], base=0, channel_multiplier=0))
            tid = tokid[:, :].rearrange("p (b t) -> p b t", t=NT)
            step(nc.gpsimd.iota(tid[:, :, 0:NX], pattern=[[S, B], [P, NX]], base=SEQ, channel_multiplier=1))
            step(nc.gpsimd.iota(tid[:, :, NX], pattern=[[S, B]], base=1, channel_multiplier=1))
            step(nc.gpsimd.iota(tid[NPATCH:SEQ, :, NX], pattern=[[S, B]], base=0, channel_multiplier=0))
            nc.gpsimd.memset(valid[:, :], 1.0).then_inc(pool_step, 1)
            n_step[0] += 1
            pool.wait_ge(pool_step, n_step[0])
            nc.gpsimd.affine_select(out=valid[:, NX::NT], in_=valid[:, NX::NT], compare_op=ALU.is_gt, fill=0.0,
                                    base=SEQ, pattern=[[0, B]], channel_multiplier=-1).then_inc(consts_ready, 1)
            rs = rstd[:, :].rearrange("p (b t) -> p b t", t=NT)
            vs = var[:, :].rearrange("p (b t) -> p b t", t=NT)
            hs = half[:, :].rearrange("p (b t) -> p b t", t=NT)
            for n, part in enumerate((slice(0, NX), slice(NX, NT))):
                pool.wait_ge(stat_ready, n + 1)
                nc.gpsimd.tensor_tensor(rs[:, :, part], vs[:, :, part], hs[:, :, part], ALU.pow).then_inc(rstd_ready, 1)
            pool.wait_ge(normed, 2)
            pool.wait_ge(ld_small, 160)
            nc.gpsimd.tensor_tensor(y_all[:, :, :], xn_all[:, :, :],
                                    boS[:, :].unsqueeze(1).to_broadcast([P, TILES, D]), ALU.add).then_inc(y_init, 1)
            pool.wait_ge(pre_evac, 7 + B)
            with pool.Fori(0, B) as b:
                at_step = pool.snap(b * STEPS)
                pool.wait_ge(q_psum, b * NT + 1)
                nc.gpsimd.tensor_copy(xs[:, :], xT_all[:, bass.ds(b, 1), :].rearrange("p a n -> p (a n)"))\
                    .then_inc(xs_ready, 1)
                for g in range(STEPS):
                    pool.wait_ge(rden_done, at_step + (g + 1))
                    if g >= 2:
                        pool.wait_ge(p_turned, at_step + (g - 1))
                    settle_pool()
                    nc.gpsimd.tensor_scalar(pn[:, g % 2, 0:S], prob[:, g % 2, :], rden[:, g % 2:g % 2 + 1], 1.0,
                                            ALU.mult, ALU.mult).then_inc(p_normed, 1)
            for n in range(2):
                pool.wait_ge(stat_ready, n + 3)
                nc.gpsimd.tensor_tensor(rstd[:, :], var[:, :], half[:, :], ALU.pow).then_inc(rstd_ready, 1)
            pool.wait_ge(slots_ready, 1)
            pool.wait_ge(ld_blank, 16)
            for t in range(TILES):
                nc.gpsimd.indirect_dma_start(
                    out=by_expert[:, :], out_offset=bass.IndirectOffsetOnAxis(ap=slotu[:, t:t + 1], axis=0),
                    in_=rows[:, t, :], in_offset=None, bounds_check=SORTED * P - 1, oob_is_err=False)\
                    .then_inc(rows_out, 16)
            with pool.Fori(0, SORTED // UN) as u:
                at_u = pool.snap(u * UN)
                for s in range(UN):
                    pool.wait_ge(yo_ready, at_u + (s + 1))
                    settle_pool()
                    nc.gpsimd.indirect_dma_start(
                        out=out_rows, out_offset=bass.IndirectOffsetOnAxis(
                            ap=ring[:, s, 2 * D + 1:2 * D + 2].bitcast(U32), axis=0),
                        in_=yo[:, s, :], in_offset=None, bounds_check=TOKENS - 1, oob_is_err=False)\
                        .then_inc(out_done[s], 16)
            for s in range(UN):
                pool.wait_ge(out_done[s], 16 * (SORTED // UN))

        @block.vector
        def _(dve):
            dve.sem_inc(gelu_done)
            dve.sem_inc(down_done)
            n_step = [0]

            def settle_vec():
                dve.sem_inc(settled_vec)


            def step(ins):
                n_step[0] += 1
                ins.then_inc(vec_step, 1)
                dve.wait_ge(vec_step, n_step[0])

            h_v = h_all[:, :, :].rearrange("p (b t) d -> p b t d", t=NT)
            xn_v = xn_all[:, :, :].rearrange("p (b t) d -> p b t d", t=NT)
            sq_v = xT_all[:, :, :].rearrange("p b (t d) -> p b t d", t=NT)
            mean_v = mean[:, :].rearrange("p (b t) -> p b t", t=NT)
            var_v = var[:, :].rearrange("p (b t) -> p b t", t=NT)
            rstd_v = rstd[:, :].rearrange("p (b t) -> p b t", t=NT)

            def wide(a, like):
                return a.unsqueeze(len(a.shape)).to_broadcast(list(like.shape))

            def normalise(n, src, cen, sq, m, v, r, eps, last=None):
                step(nc.vector.tensor_reduce(m, src, AX.X, ALU.add))
                step(nc.vector.tensor_scalar(m, m, 1.0 / D, None, ALU.mult))
                nc.vector.tensor_tensor(cen, src, wide(m, src), ALU.subtract).then_inc(centred, 1)
                dve.wait_ge(squared, n)
                step(nc.vector.tensor_reduce(v, sq, AX.X, ALU.add))
                nc.vector.tensor_scalar(v, v, 1.0 / D, eps, ALU.mult, ALU.add).then_inc(stat_ready, 1)
                dve.wait_ge(rstd_ready, n)
                nc.vector.tensor_tensor(cen, cen, wide(r, src), ALU.mult).then_inc(normed, 1)
                dve.wait_ge(normed, n)

            step(nc.vector.memset(h_v[NPATCH:P, :, NX, :], 0.0))
            step(nc.vector.memset(PTf[:, NX * P:NT * P], 0.0))
            step(nc.vector.memset(pn[:, :, S:NT * P], 0.0))
            dve.wait_ge(ld_txt, 16 * B)
            normalise(1, h_v[:, :, 0:NX, :], xn_v[:, :, 0:NX, :], sq_v[:, :, 0:NX, :],
                      mean_v[:, :, 0:NX], var_v[:, :, 0:NX], rstd_v[:, :, 0:NX], 1e-5)
            dve.wait_ge(ld_small, 160)
            step(nc.vector.tensor_tensor(h_v[NPATCH:SEQ, :, NX, :],
                                         clsS[NPATCH:SEQ, :].unsqueeze(1).to_broadcast([1, B, D]),
                                         posS[NPATCH:SEQ, :].unsqueeze(1).to_broadcast([1, B, D]), ALU.mult))
            dve.wait_ge(pre_fill, 8)
            step(nc.vector.tensor_tensor(h_v[0:NPATCH, :, NX, :],
                                         O[0:NPATCH, :].rearrange("p (b d) -> p b d", b=B),
                                         posS[0:NPATCH, :].unsqueeze(1).to_broadcast([NPATCH, B, D]), ALU.mult))
            normalise(2, h_v[:, :, NX, :], xn_v[:, :, NX, :], sq_v[:, :, NX, :],
                      mean_v[:, :, NX], var_v[:, :, NX], rstd_v[:, :, NX], 1e-5)

            dve.wait_ge(y_init, 1)
            with dve.Fori(0, B) as b:
                at_fill = dve.snap(b * FILLS)
                at_step = dve.snap(b * STEPS)
                at_tile = dve.snap(b * NT)
                at_head = dve.snap(b * H)
                at_slot = [dve.snap(b * PER_SLOT[0]), dve.snap(b * PER_SLOT[1])]
                for h in range(H):
                    dve.wait_ge(kh_done, at_head + (h + 1))
                    nc.vector.tensor_tensor(KL[:, h, :], slots[h % 2][:, 0:SP], KH[:, h, :].bitcast(F32), ALU.subtract)\
                        .then_inc(free[h % 2], 1)
                for t in range(1, NT, 2):
                    n = FIRST_V + t
                    dve.wait_ge(filled, at_fill + (n + 1))
                    nc.vector.tensor_copy(Vt[:, t, :], slots[n % 2]).then_inc(free[n % 2], 1)

                def queries(t):
                    for par in range(2):
                        dve.wait_ge(q_hi, (at_tile + t) * 2 + 2)
                        nc.vector.tensor_tensor(QS[K:2 * K, t % 2, par::2, :],
                                                Q[K * par:K * par + K, :].rearrange("p (i m) -> p i m", m=P),
                                                QS[0:K, t % 2, par::2, :].bitcast(F32), ALU.subtract).then_inc(q_lo, 1)

                queries(0)

                def reciprocals(g):
                    dve.wait_ge(exp_done, at_step + (g + 1))
                    if g >= 2:
                        dve.wait_ge(p_normed, at_step + (g - 1))
                    nc.vector.reciprocal(rden[:, g % 2:g % 2 + 1], den[:, g % 2:g % 2 + 1]).then_inc(rden_done, 1)

                def mask_and_max(g):
                    n = FIRST_S + g
                    sc = slots[n % 2][:, 0:S]
                    dve.wait_ge(filled, at_fill + (n + 1))
                    if g >= 1:
                        m = n - 1
                        dve.wait_ge(free[m % 2], at_slot[m % 2] + (m // 2 + 2))
                    nc.vector.tensor_scalar(zero_mark[:, :], sc, 0.0, -1e9 * K ** 0.5, ALU.is_equal, ALU.mult)\
                        .then_inc(z_done, 1)
                    if g >= 2:
                        dve.wait_ge(exp_done, at_step + (g - 1))
                    if g >= 1:
                        reciprocals(g - 1)
                    dve.wait_ge(z_done, at_step + (g + 1))
                    settle_vec()
                    nc.vector.tensor_tensor_reduce(sneg[:, g % 2, :], sc, zero_mark[:, :], -(K ** -0.5), 3e38,
                                                   ALU.add, ALU.min, rmax[:, g % 2:g % 2 + 1]).then_inc(free[n % 2], 1)

                def finish_tile(t):
                    dve.wait_ge(pv_done, at_step + H * (t + 1))
                    y = y_all[:, bass.ds(at_tile + t, 1), :].rearrange("p a d -> p (a d)")
                    nc.vector.tensor_tensor(y, O[:, 0:D], y, ALU.add).then_inc(y_done, 1)

                for g in range(STEPS):
                    mask_and_max(g)
                    if g % H == QSTEP and g // H + 1 < NT:
                        queries(g // H + 1)
                    if g % H == 2 and g >= H:
                        finish_tile(g // H - 1)
                reciprocals(STEPS - 1)
                finish_tile(NT - 1)

            dve.wait_ge(y_done, TILES + 1)
            sq = xT_all[:, :, :].rearrange("p b (t d) -> p (b t) d", t=NT)
            normalise(3, y_all[:, :, :], xn_all[:, :, :], sq, mean[:, :], var[:, :], rstd[:, :], 1e-6)
            for vec, op in ((gammaS, ALU.mult), (betaS, ALU.add)):
                step(nc.vector.tensor_tensor(xn_all[:, :, :], xn_all[:, :, :],
                                             vec[:, :].unsqueeze(1).to_broadcast([P, TILES, D]), op))
            step(nc.vector.tensor_tensor(rows[:, :, 0:D], xn_all[:, :, :], h_all[:, :, :], ALU.add))
            normalise(4, rows[:, :, 0:D], rows[:, :, D:2 * D], xn_all[:, :, :],
                      mean[:, :], var[:, :], rstd[:, :], 1e-5)

            dve.wait_ge(consts_ready, 3)
            step(nc.vector.tensor_copy(ramp[:, :], rampi[:, :]))
            step(nc.vector.tensor_scalar(rampP[:, :], ramp[:, :], float(P), None, ALU.mult))
            step(nc.vector.tensor_scalar(order[:, :], ramp[:, 0:E], -1.0, float(E), ALU.mult, ALU.add))
            step(nc.vector.memset(fresh[:, :, :], 1.0))
            step(nc.vector.memset(fresh[:, :, 0:1], 0.0))
            step(nc.vector.memset(one8[:, :], 1.0))

            dve.wait_ge(logits_done, 1)
            lg = Q[:, 0:TILES * E].rearrange("p (t e) -> p t e", e=E)
            step(nc.vector.tensor_tensor(logit[:, :, :], lg, bsS[:, :].unsqueeze(1).to_broadcast([P, TILES, E]), ALU.add))
            step(nc.vector.tensor_reduce(lmax[:, :], logit[:, :, :], AX.X, ALU.max))
            nc.vector.tensor_tensor(psel[:, :, :], logit[:, :, :], wide(lmax[:, :], logit[:, :, :]), ALU.subtract)\
                .then_inc(l_ready, 1)
            hot_t = hot[:, :, :].rearrange("p e t -> p t e")
            step(nc.vector.tensor_tensor(hot_t, logit[:, :, :], wide(lmax[:, :], logit[:, :, :]), ALU.is_equal))
            step(nc.vector.tensor_tensor(hot_t, hot_t, order[:, :].unsqueeze(1).to_broadcast([P, TILES, E]), ALU.mult))
            step(nc.vector.tensor_reduce(slotf[:, :], hot_t, AX.X, ALU.max))
            step(nc.vector.tensor_tensor(hot_t, order[:, :].unsqueeze(1).to_broadcast([P, TILES, E]),
                                         wide(slotf[:, :], logit[:, :, :]), ALU.is_equal))
            nc.vector.tensor_tensor(hot_t, hot_t, wide(valid[:, :], logit[:, :, :]), ALU.mult).then_inc(hot_ready, 1)
            dve.wait_ge(l_exp, 1)
            step(nc.vector.tensor_reduce(psum_[:, :], psel[:, :, :], AX.X, ALU.add))
            step(nc.vector.reciprocal(pbest[:, :], psum_[:, :]))
            step(nc.vector.tensor_copy(rows[:, :, 2 * D], pbest[:, :]))
            step(nc.vector.tensor_copy(rows[:, :, 2 * D + 1].bitcast(I32), tokid[:, :]))
            step(nc.vector.memset(rows[:, :, 2 * D + 2:ROW], 0.0))

            dve.wait_ge(ranks_done, 1)
            rank = O[:, 0:E * TILES].rearrange("p (e t) -> p e t", e=E)
            count = PT[:, 1, 0:E * TILES]
            flat = "p e t -> p (e t)"
            step(nc.vector.tensor_tensor_scan(incl[:, :, :].rearrange(flat), fresh[:, :, :].rearrange(flat), count, 0.0,
                                              ALU.mult, ALU.add))
            step(nc.vector.tensor_tensor(base[:, :, :].rearrange(flat), incl[:, :, :].rearrange(flat), count,
                                         ALU.subtract))
            cm = cmp[:, 0:E * TILES].rearrange("p (e t) -> p e t", e=E)
            step(nc.vector.tensor_tensor(cm, incl[:, :, TILES - 1:TILES].to_broadcast([P, E, TILES]),
                                         rampP[:, 0:TILES].unsqueeze(1).to_broadcast([P, E, TILES]), ALU.is_gt))
            step(nc.vector.tensor_reduce(ntile[:, :], cm, AX.X, ALU.add))
            step(nc.vector.tensor_tensor_scan(tend[:, :], one8[:, :], ntile[:, :], 0.0, ALU.mult, ALU.add))
            ce = cmp[:, 0:SORTED * E].rearrange("p (i e) -> p i e", e=E)
            step(nc.vector.tensor_tensor(ce, wide(ramp[:, 0:SORTED], ce),
                                         tend[:, :].unsqueeze(1).to_broadcast([P, SORTED, E]), ALU.is_ge))
            step(nc.vector.tensor_reduce(exf[:, :], ce, AX.X, ALU.add))
            step(nc.vector.tensor_scalar(exf[:, :], exf[:, :], float(E - 1), None, ALU.min))
            nc.vector.tensor_copy(exi[:, :], exf[:, :]).then_inc(experts_ready, 1)
            step(nc.vector.tensor_tensor(tend[:, :], tend[:, :], ntile[:, :], ALU.subtract))
            step(nc.vector.tensor_scalar(tend[:, :], tend[:, :], float(P), None, ALU.mult))
            step(nc.vector.tensor_tensor(base[:, :, :], base[:, :, :], wide(tend[:, :], base[:, :, :]), ALU.add))
            step(nc.vector.tensor_tensor(base[:, :, :], rank, base[:, :, :], ALU.add))
            step(nc.vector.tensor_tensor(base[:, :, :], base[:, :, :], hot[:, :, :], ALU.mult))
            step(nc.vector.tensor_reduce(slotf[:, :], base[:, :, :].rearrange("p e t -> p t e"), AX.X, ALU.add))
            step(nc.vector.tensor_scalar(lmax[:, :], valid[:, :], -float(SKIP), float(SKIP), ALU.mult, ALU.add))
            step(nc.vector.tensor_tensor(slotf[:, :], slotf[:, :], lmax[:, :], ALU.add))
            nc.vector.tensor_copy(slotu[:, :], slotf[:, :]).then_inc(slots_ready, 1)

            dve.wait_ge(experts_ready, 1)
            dve.wait_ge(ld_experts, 48)
            with dve.Fori(0, SORTED // UN) as u:
                at_u = dve.snap(u * UN)

                def up(s, e):
                    dve.wait_ge(up_done, at_u + (s + 2))
                    dve.wait_ge(gelu_done, at_u + (max(s - 1, 0) + 1))
                    nc.vector.tensor_tensor(hid[:, s % 2, :], SL[:, s % 2, :], b1S[:, bass.ds(e * FF, FF)], ALU.add)\
                        .then_inc(up_biased, 1)

                def turned(s):
                    dve.wait_ge(hid_turned, at_u + (s + 2))
                    dve.wait_ge(down_done, at_u + (max(s - 1, 0) + 1))
                    nc.vector.tensor_copy(hidT[:, s % 2, :], SL[:, 2 + s % 2, :]).then_inc(hidT_ready, 1)

                def down(s, e):
                    dve.wait_ge(down_done, at_u + (s + 2))
                    dve.wait_ge(row_in[s], u * 16 + 16)
                    nc.vector.tensor_tensor(yo[:, s, :], PT[:, s % 2, 0:D], b2S[:, bass.ds(e * D, D)], ALU.add)\
                        .then_inc(yb_done, 1)
                    dve.wait_ge(yb_done, at_u + (s + 2))
                    nc.vector.scalar_tensor_tensor(out=yo[:, s, :], in0=yo[:, s, :],
                                                   scalar=ring[:, s, 2 * D:2 * D + 1], in1=ring[:, s, 0:D],
                                                   op0=ALU.mult, op1=ALU.add).then_inc(yo_ready, 1)

                es = []
                for s in range(UN):
                    es.append(dve.value_load(exi[0:1, bass.ds(at_u + s, 1)], min_val=0, max_val=E - 1))
                for s in range(UN):
                    up(s, es[s])
                    if s >= 1:
                        turned(s - 1)
                        down(s - 1, es[s - 1])
                turned(UN - 1)
                down(UN - 1, es[UN - 1])

        @block.tensor
        def _(pe):
            for primed in (*free, q_lo, y_done, fT_ready, up_biased, hidT_ready, yb_done):
                pe.sem_inc(primed)
            pe.wait_ge(consts_ready, 1)
            pe.wait_ge(ld_attn, 16 * 5)
            for h in range(H):
                last = nc.tensor.transpose(slots[0][:, h * D:(h + 1) * D], WvS[:, h * D:(h + 1) * D], ident[:, :])
            last.then_inc(pre_fill, 1)
            pe.wait_ge(pre_evac, 1)
            for h in range(H):
                last = nc.tensor.matmul(slots[1][:, h * D:(h + 1) * D], WvT[:, h * D:(h + 1) * D], WoS[:, h, :],
                                        start=True, stop=True)
            last.then_inc(pre_fill, 1)
            pe.wait_ge(ld_tok, 16 * (1 + B * C))
            for g in range(4):
                n = min(8, PX - 8 * g)
                pe.wait_ge(pre_evac, g + 1)
                for j in range(n):
                    last = nc.tensor.transpose(slots[g % 2][0:CI, j * D:(j + 1) * D], WtS[:, 8 * g + j::PX], ident[:, :])
                last.then_inc(pre_fill, 1)
            pe.wait_ge(pre_evac, 6)
            Xv = X.rearrange("p g (w j) -> p g w j", j=PX)
            for j in range(PX):
                last = nc.tensor.matmul(Q[:, 0:B * NPATCH].rearrange("p (g w) -> p g w", w=GRID), WtT[:, j, :], Xv[:, :, :, j],
                                        start=(j == 0), stop=(j == PX - 1))
            last.then_inc(pre_fill, 1)
            pe.wait_ge(pre_evac, 7)
            for b in range(B):
                last = nc.tensor.transpose(O[0:NPATCH, b * D:(b + 1) * D], tokT[:, b * NPATCH:(b + 1) * NPATCH],
                                           ident[:, :])
            last.then_inc(pre_fill, 1)
            pe.wait_ge(normed, 2)
            for b in range(B):
                if b >= 2:
                    pe.wait_ge(pre_evac, 6 + b)
                for t in range(NT):
                    last = nc.tensor.transpose(slots[b % 2][:, t * P:(t + 1) * P], xn_all[:, b * NT + t, :], ident[:, :])
                last.then_inc(pre_fill, 1)

            pe.wait_ge(pre_evac, 7 + B)
            with pe.Fori(0, B) as b:
                at_step = pe.snap(b * STEPS)
                at_tile = pe.snap(b * NT)
                at_slot = [pe.snap(b * PER_SLOT[0]), pe.snap(b * PER_SLOT[1])]

                def wait_slot(n):
                    pe.wait_ge(free[n % 2], at_slot[n % 2] + (n // 2 + 1))

                def queries(t):
                    pe.wait_ge(q_lo, (at_tile + t) * 2 + 1)
                    for i in range(H // 2):
                        last = nc.tensor.matmul(Q[:, i * P:(i + 1) * P], WqS[:, i * P:(i + 1) * P],
                                                xs[:, t * P:(t + 1) * P], start=True, stop=True)
                    last.then_inc(q_psum, 1)

                def scores(g):
                    t, h = divmod(g, H)
                    n = FIRST_S + g
                    wait_slot(n)
                    if h == 0:
                        pe.wait_ge(q_lo, (at_tile + t) * 2 + 3)
                    for a, c in ((0, 512), (512, SP)):
                        for part, keys in enumerate((KH, KL)):
                            last = nc.tensor.matmul(slots[n % 2][:, a:c], QS[:, t % 2, h, :], keys[:, h, a:c],
                                                    start=(part == 0), stop=(part == 1))
                    last.then_inc(filled, 1)

                def turn(g):
                    pe.wait_ge(p_normed, at_step + (g + 1))
                    if g >= 1:
                        pe.wait_ge(pt_evac, at_step + g)
                    for t in range(NT):
                        n = P if t < NX else TAIL
                        last = nc.tensor.transpose(PTf[0:n, t * P:(t + 1) * P], pn[:, g % 2, t * P:t * P + n], ident[:, :])
                    last.then_inc(p_turned, 1)

                def values(g):
                    tile, h = divmod(g, H)
                    pe.wait_ge(pt_evac, at_step + (g + 1))
                    if h == 0:
                        pe.wait_ge(y_done, at_tile + (tile + 1))
                    for t in range(NT):
                        n = P if t < NX else TAIL
                        last = nc.tensor.matmul(O[:, 0:D], pT[0:n, g % 2, t * P:(t + 1) * P],
                                                Vt[0:n, t, h * D:(h + 1) * D],
                                                start=(h == 0 and t == 0), stop=(h == H - 1 and t == NX))
                    last.then_inc(pv_done, 1)

                pe.wait_ge(xs_ready, b + 1)
                for h in range(H):
                    wait_slot(h)
                    for a, c in ((0, 512), (512, SP)):
                        last = nc.tensor.matmul(slots[h % 2][:, a:c], WkS[:, h, :, :].rearrange("p a k -> p (a k)"), xs[:, a:c],
                                                start=True, stop=True)
                    last.then_inc(filled, 1)
                queries(0)
                for t in range(NT):
                    n = FIRST_V + t
                    wait_slot(n)
                    for c in range(2):
                        last = nc.tensor.matmul(slots[n % 2][:, c * 512:(c + 1) * 512], xs[:, t * P:(t + 1) * P],
                                                VO[:, c * 512:(c + 1) * 512], start=True, stop=True)
                    last.then_inc(filled, 1)
                pe.wait_ge(free[FIRST_S % 2 ^ 1], at_slot[FIRST_S % 2 ^ 1] + ((FIRST_S + 1) // 2 + 1))
                scores(0)
                scores(1)
                for g in range(STEPS):
                    if g % H == QSTEP and g // H + 1 < NT:
                        queries(g // H + 1)
                    if g + 2 < STEPS:
                        scores(g + 2)
                    if g >= 1:
                        turn(g - 1)
                    if g >= 2:
                        values(g - 2)
                turn(STEPS - 1)
                values(STEPS - 2)
                values(STEPS - 1)

            pe.wait_ge(normed, 4)
            pe.wait_ge(y_done, TILES + 1)
            for q in range(NT):
                if q >= 2:
                    pe.wait_ge(r_evac, q - 1)
                for c in range(4):
                    last = nc.tensor.transpose(SL[:, q % 2, c * P:(c + 1) * P], rows[:, 4 * q + c, D:2 * D], ident[:, :])
                last.then_inc(r_fill, 1)
            xt = xT_all[:, :, :].rearrange("p b n -> p (b n)")
            pe.wait_ge(r_evac, NT)
            for t in range(TILES):
                last = nc.tensor.matmul(Q[:, t * E:(t + 1) * E], xt[:, t * P:(t + 1) * P], WsS[:, :], start=True, stop=True)
            last.then_inc(logits_done, 1)
            pe.wait_ge(hot_ready, 1)
            flat_hot = hot[:, :, :].rearrange("p e t -> p (e t)")
            nc.tensor.matmul(O[:, 0:E * TILES], before[:, :], flat_hot, start=True, stop=True)
            nc.tensor.matmul(PT[:, 1, 0:E * TILES], ones[:, :], flat_hot, start=True, stop=True).then_inc(ranks_done, 1)

            pe.wait_ge(experts_ready, 1)
            pe.wait_ge(slots_ready, 1)
            pe.wait_ge(ld_experts, 48)
            with pe.Fori(0, SORTED // UN) as u:
                at_u = pe.snap(u * UN)

                def turn_rows(s):
                    pe.wait_ge(row_in[s], u * 16 + 16)
                    pe.wait_ge(fT_ready, at_u + (s + 1))
                    nc.tensor.transpose(Q[:, 0:P], ring[:, s, D:2 * D], ident[:, :]).then_inc(f_turned, 1)

                def up(s, e):
                    pe.wait_ge(fT_ready, at_u + (s + 2))
                    pe.wait_ge(up_biased, at_u + (max(s - 1, 0) + 1))
                    nc.tensor.matmul(SL[:, s % 2, :], fT[:, s % 2, :], W1S[:, bass.ds(e * FF, FF)],
                                     start=True, stop=True).then_inc(up_done, 1)

                def turn_hidden(s):
                    pe.wait_ge(gelu_done, at_u + (s + 2))
                    pe.wait_ge(hidT_ready, at_u + (max(s - 1, 0) + 1))
                    for c in range(NF):
                        last = nc.tensor.transpose(SL[:, 2 + s % 2, c * P:(c + 1) * P],
                                                   act_h[:, s % 2, c * P:(c + 1) * P], ident[:, :])
                    last.then_inc(hid_turned, 1)

                def down(s, e):
                    pe.wait_ge(hidT_ready, at_u + (s + 2))
                    pe.wait_ge(yb_done, at_u + (max(s - 1, 0) + 1))
                    for c in range(NF):
                        last = nc.tensor.matmul(PT[:, s % 2, 0:D], hidT[:, s % 2, c * P:(c + 1) * P],
                                                W2S[:, bass.ds(e * (NF * D) + c * D, D)],
                                                start=(c == 0), stop=(c == NF - 1))
                    last.then_inc(down_done, 1)

                es = []
                for s in range(UN):
                    es.append(pe.value_load(exi[0:1, bass.ds(at_u + s, 1)], min_val=0, max_val=E - 1))
                turn_rows(0)
                for s in range(UN):
                    up(s, es[s])
                    if s + 1 < UN:
                        turn_rows(s + 1)
                    if s >= 1:
                        turn_hidden(s - 1)
                        down(s - 1, es[s - 1])
                turn_hidden(UN - 1)
                down(UN - 1, es[UN - 1])


QSTEP = 3

_INS = ['x', 'txt', 'L0_tok_W', 'L0_tok_b', 'L0_tok_class_token', 'L0_tok_pos_embed', 'L0_attn_Wq', 'L0_attn_Wk',
        'L0_attn_Wv', 'L0_attn_Wo', 'L0_attn_bo', 'L0_attn_gamma', 'L0_attn_beta', 'L0_ffn_Ws', 'L0_ffn_bs',
        'L0_ffn_W1', 'L0_ffn_b1', 'L0_ffn_W2', 'L0_ffn_b2']


def kernel(**inputs):
    import numpy as _np
    import concourse.bacc as _bacc
    from concourse import mybir as _mybir
    from concourse.bass_utils import run_bass_kernel_spmd as _run

    nc = _bacc.Bacc("TRN2", target_bir_lowering=False, num_devices=1)
    arrays, args = {}, []
    for name in _INS:
        a = _np.ascontiguousarray(inputs[name])
        arrays[f"in_{name}_dram"] = a
        args.append(nc.dram_tensor(f"in_{name}_dram", a.shape, _mybir.dt.from_np(a.dtype), kind="ExternalInput").ap())
    B, C, IMG, _ = inputs['x'].shape
    NTXT, D = inputs['txt'].shape[1:]
    S = inputs['L0_tok_pos_embed'].shape[0] + NTXT
    E = inputs['L0_ffn_Ws'].shape[1]
    out = nc.dram_tensor("out_0_dram", (B, S, D), _mybir.dt.float32, kind="ExternalOutput").ap()
    n_sorted = ((B * S - E) // 128 + E) * 128
    by_expert = nc.dram_tensor("rows_by_expert", (n_sorted, 2 * D + 4), _mybir.dt.float32, kind="Internal").ap()
    early_fusion_kernel(nc, *args, out, by_expert)
    r = _run(nc, [arrays], core_ids=[0])
    return r.results[0]["out_0_dram"]
```

```python
from contextlib import ExitStack

import concourse.bass as bass
from concourse import mybir

F32 = mybir.dt.float32
F32R = mybir.dt.float32r
I32 = mybir.dt.int32
U32 = mybir.dt.uint32
ALU = mybir.AluOpType
ACT = mybir.ActivationFunctionType
AX = mybir.AxisListType

P = 128


def early_fusion_kernel(
    nc, x, txt, tok_W, tok_b, cls_tok, pos, Wq, Wk, Wv, Wo, bo, gamma, beta, Ws, bs, W1, b1, W2, b2, out, by_expert,
):
    B, C, IMG, _ = x.shape
    D = txt.shape[2]
    NTXT = txt.shape[1]
    SEQ = pos.shape[0]
    NPATCH = SEQ - 1
    GRID = int(round(NPATCH ** 0.5))
    PX = IMG // GRID
    CI = C * PX
    S = SEQ + NTXT
    K = 64
    H = Wq.shape[1] // K
    NX = NTXT // P
    NT = NX + 1
    TILES = B * NT
    SP = S + 1
    TAIL = SEQ
    E = Ws.shape[1]
    FF = W1.shape[2]
    NF = FF // P
    TOKENS = B * S
    SORTED = (TOKENS - E) // P + E
    MEAN, RSTD, PBEST, TOKEN = range(D, D + 4)
    ROW = D + 4
    SKIP = 1 << 20
    UN = 3
    AHEAD = 4
    LOOPED = (SORTED - AHEAD) // UN
    assert D == P and NX * P == NTXT and SEQ <= P and H * K == 4 * P

    STEPS = NT * H
    fills = [("keys", h) for h in range(H)] + [("scores", 0), ("scores", 1)]
    fills += [("values", t) for t in range(NT)] + [("scores", g) for g in range(2, STEPS)]
    FILL = {fill: n for n, fill in enumerate(fills)}
    FILLS = len(fills)
    PER_SLOT = [(FILLS + 1) // 2, FILLS // 2]

    with ExitStack() as ctx:
        def sb(name, shape, dt=F32):
            return ctx.enter_context(nc.sbuf_tensor(name, shape, dt))

        def psum(name, shape):
            return ctx.enter_context(nc.psum_tensor(name, shape, F32))

        def sem(name):
            return ctx.enter_context(nc.semaphore(name))

        ident = sb("ident", [P, P])
        ones = sb("ones", [P, P])
        before = sb("before", [P, P])
        h_row = sb("h_row", [P, TILES + 1, ROW])
        h_all = h_row[:, 1:, 0:D]
        y_row = sb("y_row", [P, TILES + 1, D])
        y_all = y_row[:, 1:, :]
        xn_all = sb("xn_all", [P, TILES, D])
        xT_all = sb("xT_all", [P, B + 1, NT * P])
        xs = sb("xs", [P, NT * P])
        WqS = sb("WqS", [P, H * K])
        WkS = sb("WkS", [P, H, 2, K])
        VO = sb("VO", [P, H * D])
        KH = sb("KH", [P, H, SP], F32R)
        KL = sb("KL", [P, H, SP], F32R)
        QS = sb("QS", [P, 2, H, P], F32R)
        V = sb("V", [P, NT * H * D])
        Vt = V[:, :].rearrange("p (t n) -> p t n", t=NT)
        WvT = V[:, 0:H * D]
        WvS = V[:, H * D:2 * H * D]
        WoS = V[:, 2 * H * D:3 * H * D].rearrange("p (h d) -> p h d", h=H)
        score = sb("score", [P, 2, S])
        zero_mark = sb("zero_mark", [P, S])
        rmax = sb("rmax", [P, 2])
        prob = sb("prob", [P, 2, S])
        den = sb("den", [P, 2])
        rden = sb("rden", [P, 2])
        pn = sb("pn", [P, 2, NT * P])
        pT = sb("pT", [P, 2, NT * P])
        stage = sb("stage", [P, max(B * GRID * IMG + C * PX * PX + PX * D, 3 * E * FF)])
        X = stage[0:CI, 0:B * GRID * IMG].rearrange("p (g w) -> p g w", w=IMG)
        at = B * GRID * IMG
        WtS = stage[:, at:at + C * PX * PX]
        at += C * PX * PX
        WtT = stage[0:CI, at:at + PX * D].rearrange("p (j d) -> p j d", d=D)
        W1S = stage[:, 0:E * FF]
        W2S = stage[:, E * FF:2 * E * FF]
        b1S = stage[:, 2 * E * FF:3 * E * FF]
        b2S = sb("b2S", [P, E * D])
        tokT = sb("tokT", [P, B * NPATCH])
        posS = sb("posS", [P, D])
        clsS = sb("clsS", [P, D])
        boS = sb("boS", [P, D])
        gammaS = sb("gammaS", [P, D])
        betaS = sb("betaS", [P, D])
        tbS = sb("tbS", [P, 1])
        WsS = sb("WsS", [P, E])
        bsS = sb("bsS", [P, E])
        mean = sb("mean", [P, TILES])
        var = sb("var", [P, TILES])
        rstd = sb("rstd", [P, TILES])
        half = sb("half", [P, TILES])
        eps2 = sb("eps2", [P, 2])
        six = sb("six", [P, 6])
        stat = sb("stat", [P, 2])
        stat3 = sb("stat3", [P, 2])
        spread = sb("spread", [P, 2])
        scaled = sb("scaled", [P, D])
        x3 = sb("x3", [P, D])
        x3T = sb("x3T", [P, D])
        lg_row = sb("lg_row", [P, TILES + 2, E])
        idx = sb("idx", [P, UN], U32)
        tokid = sb("tokid", [P, TILES], I32)
        spare = prob[:, :, :].rearrange("p a n -> p (a n)")
        RT = E * TILES
        logit, psel = (spare[:, n * RT:(n + 1) * RT].rearrange("p (t e) -> p t e", e=E) for n in range(2))
        fresh, incl, base = (spare[:, n * RT:(n + 1) * RT].rearrange("p (e t) -> p e t", e=E) for n in range(2, 5))
        cmp = spare[:, 5 * RT:5 * RT + SORTED * E]
        lmax = sb("lmax", [P, TILES])
        psum_ = sb("psum_", [P, TILES])
        pbest = sb("pbest", [P, TILES])
        hot = sb("hot", [P, E, TILES])
        order = sb("order", [P, E])
        ramp = sb("ramp", [P, 32])
        rampi = sb("rampi", [P, 32], I32)
        rampP = sb("rampP", [P, 32])
        ntile = sb("ntile", [P, E])
        tend = sb("tend", [P, E])
        one8 = sb("one8", [P, E])
        valid = sb("valid", [P, TILES])
        slotf = sb("slotf", [P, TILES])
        slotu = sb("slotu", [P, TILES], U32)
        exf = sb("exf", [P, SORTED])
        exi = sb("exi", [P, SORTED], I32)
        blank = sb("blank", [P, ROW])
        sorted_in = V[:, 0:SORTED * ROW].rearrange("p (i c) -> p i c", c=ROW)
        at = SORTED * ROW
        hidT = V[:, at:at + UN * FF].rearrange("p (s f) -> p s f", s=UN)
        y_flat = y_row[:, :, :].rearrange("p t d -> p (t d)")
        xf, fT, yo = (y_flat[:, n * UN * D:(n + 1) * UN * D].rearrange("p (s d) -> p s d", s=UN) for n in range(3))
        hid = xn_all[:, :, :].rearrange("p t d -> p (t d)")[:, 0:UN * FF].rearrange("p (s f) -> p s f", s=UN)
        act_h = xT_all[:, :, :].rearrange("p b n -> p (b n)")[:, 0:UN * FF].rearrange("p (s f) -> p s f", s=UN)

        SL = psum("SL", [P, 4, 512])
        PT = psum("PT", [P, 2, 512])
        O = psum("O", [P, 512])
        Q = psum("Q", [P, 512])
        slots = [SL[:, 2 * s:2 * s + 2, :].rearrange("p a n -> p (a n)") for s in range(2)]
        PTf = PT[:, :, :].rearrange("p a n -> p (a n)")
        LG = (NT + 1) * P
        hidT_ps = [SL[:, 3, :], PT[:, 0, :], PT[:, 1, :]]

        ld_txt, ld_attn, ld_small, ld_tok, ld_experts, ld_blank = (
            sem(n) for n in ("ld_txt", "ld_attn", "ld_small", "ld_tok", "ld_experts", "ld_blank"))
        consts_ready = sem("consts_ready")
        settled_vec, settled_pool = sem("settled_vec"), sem("settled_pool")
        pool_step = sem("pool_step")
        vec_step = sem("vec_step")
        act_step = sem("act_step")
        patches_in_h = sem("patches_in_h")
        stat_ready = sem("stat_ready")
        rstd_ready = sem("rstd_ready")
        centred = sem("centred")
        squared = sem("squared")
        normed = sem("normed")
        pre_fill = sem("pre_fill")
        pre_evac = sem("pre_evac")
        y_init = sem("y_init")
        xs_ready = sem("xs_ready")
        filled = sem("filled")
        free = [sem("free0"), sem("free1")]
        kh_done = sem("kh_done")
        q_psum = sem("q_psum")
        q_hi = sem("q_hi")
        q_lo = sem("q_lo")
        z_done = sem("z_done")
        max_done = sem("max_done")
        exp_done = sem("exp_done")
        rden_done = sem("rden_done")
        p_normed = sem("p_normed")
        p_turned = sem("p_turned")
        pt_evac = sem("pt_evac")
        pv_done = sem("pv_done")
        y_done = sem("y_done")
        six_done, stat_done, rstd3_done, spread_done = (sem(n) for n in ("six_done", "stat_done", "rstd3_done", "spread_done"))
        scaled_done, h_done, x3_done, x3_turned, x3_evac = (
            sem(n) for n in ("scaled_done", "h_done", "x3_done", "x3_turned", "x3_evac"))
        stat_kept = sem("stat_kept")
        lg_done, lg_evac = sem("lg_done"), sem("lg_evac")
        l_ready = sem("l_ready")
        l_exp = sem("l_exp")
        hot_ready = sem("hot_ready")
        ranks_done = sem("ranks_done")
        slots_ready = sem("slots_ready")
        experts_ready = sem("experts_ready")
        rows_out = sem("rows_out")
        rows_in = sem("rows_in")
        xf_ready, f_turned, fT_ready, up_done, up_biased = (
            sem(n) for n in ("xf_ready", "f_turned", "fT_ready", "up_done", "up_biased"))
        gelu_done, hid_turned, hidT_ready, down_done, yb_done, yo_ready = (
            sem(n) for n in ("gelu_done", "hid_turned", "hidT_ready", "down_done", "yb_done", "yo_ready"))
        out_done = [sem(f"out_done{s}") for s in range(UN)]

        out_rows = out.rearrange("b s d -> (b s) d")
        block = ctx.enter_context(nc.Block())

        def expert_tiles(eng):
            for i in range(2 * UN):
                yield i, i % UN, i // UN
            with eng.Fori(2, LOOPED) as u:
                at_u = eng.snap(u * UN)
                for s in range(UN):
                    yield at_u + s, s, u
            for i in range(LOOPED * UN, SORTED):
                yield i, i % UN, i // UN

        def later(i, n):
            return not isinstance(i, int) or i + n < SORTED

        @block.sync
        def _(sp):
            for b in range(B):
                sp.dma_start(h_row[:, b * NT + 1:b * NT + 1 + NX, 0:D],
                             txt[b].rearrange("(t p) d -> p t d", p=P)).then_inc(ld_txt, 16)
            sp.dma_start(WtS, tok_W[:, :]).then_inc(ld_tok, 16)
            for b in range(B):
                for c in range(C):
                    sp.dma_start(X[c * PX:(c + 1) * PX, b * GRID:(b + 1) * GRID, :],
                                 x[b, c].rearrange("(g i) w -> i g w", i=PX)).then_inc(ld_tok, 16)
            sp.wait_ge(pre_fill, 7)
            sp.dma_start(W1S.rearrange("p (e f) -> p e f", e=E), W1.rearrange("e d f -> d e f")).then_inc(ld_experts, 16)
            sp.dma_start(W2S.rearrange("p (e n d) -> p e n d", e=E, n=NF),
                         W2.rearrange("e (n p) d -> p e n d", p=P)).then_inc(ld_experts, 16)
            sp.dma_start(b1S, b1.rearrange("e f -> (e f)").partition_broadcast(P)).then_inc(ld_experts, 16)
            sp.wait_ge(consts_ready, 2)
            sp.dma_start(by_expert.rearrange("(t p) c -> p t c", p=P),
                         blank[:, :].unsqueeze(1).to_broadcast([P, SORTED, ROW])).then_inc(ld_blank, 16)
            sp.wait_ge(rows_out, 16 * TILES)
            for i in range(0, SORTED, 5):
                sp.dma_start(sorted_in[:, i:i + 5, :],
                             by_expert[i * P:(i + 5) * P, :].rearrange("(t p) c -> p t c", p=P)).then_inc(rows_in, 16)

        @block.scalar
        def _(act):
            act.dma_start(WvS[:, :], Wv).then_inc(ld_attn, 16)
            act.dma_start(WoS[:, :, :], Wo.rearrange("(h v) d -> v h d", v=D)).then_inc(ld_attn, 16)
            act.dma_start(posS[0:NPATCH, :], pos[1:SEQ, :]).then_inc(ld_small, 16)
            act.dma_start(posS[NPATCH:SEQ, :], pos[0:1, :]).then_inc(ld_small, 16)
            act.dma_start(clsS[NPATCH:SEQ, :], cls_tok).then_inc(ld_small, 16)
            act.dma_start(tbS[:, :], tok_b.unsqueeze(1)).then_inc(ld_small, 16)
            for t, v in ((boS, bo), (gammaS, gamma), (betaS, beta), (bsS, bs)):
                act.dma_start(t[:, :], v.partition_broadcast(P)).then_inc(ld_small, 16)
            act.dma_start(WsS[:, :], Ws).then_inc(ld_small, 16)
            act.dma_start(b2S[:, :], b2.rearrange("e d -> (e d)").partition_broadcast(P)).then_inc(ld_small, 16)
            act.dma_start(WqS[:, :], Wq).then_inc(ld_attn, 16)
            for two in range(2):
                act.dma_start(WkS[:, :, two, :], Wk.rearrange("d (h k) -> d h k", h=H)).then_inc(ld_attn, 16)

            def squares(n, src, dst):
                act.wait_ge(centred, n)
                nc.scalar.activation(dst, src, ACT.Square).then_inc(squared, 1)

            act.wait_ge(pre_fill, 1)
            nc.scalar.activation(WvT, slots[0], ACT.Copy).then_inc(pre_evac, 1)
            act.wait_ge(pre_fill, 2)
            nc.scalar.activation(VO[:, :], slots[1], ACT.Copy).then_inc(pre_evac, 1)
            sq_all = xT_all[:, 0:B, :].rearrange("p b (t d) -> p b t d", t=NT)
            xn_v = xn_all[:, :, :].rearrange("p (b t) d -> p b t d", t=NT)
            squares(1, xn_v[:, :, 0:NX, :], sq_all[:, :, 0:NX, :])
            for g in range(4):
                n = min(8, PX - 8 * g)
                act.wait_ge(pre_fill, 3 + g)
                nc.scalar.activation(WtT[:, 8 * g:8 * g + n, :].rearrange("p j d -> p (j d)"),
                                     slots[g % 2][0:CI, 0:n * D], ACT.Copy).then_inc(pre_evac, 1)
            act.wait_ge(pre_fill, 7)
            act.wait_ge(ld_small, 160)
            nc.scalar.activation(tokT[:, :], Q[:, 0:B * NPATCH], ACT.Identity, bias=tbS[:, 0:1]).then_inc(pre_evac, 1)
            squares(2, xn_v[:, :, NX, :], sq_all[:, :, NX, :])
            for b in range(B):
                act.wait_ge(pre_fill, 9 + b)
                nc.scalar.activation(xT_all[:, b, :], slots[b % 2][:, 0:NT * P], ACT.Copy).then_inc(pre_evac, 1)

            with act.Fori(0, B) as b:
                at_fill = act.snap(b * FILLS)
                at_step = act.snap(b * STEPS)
                at_tile = act.snap(b * NT)
                at_slot = [act.snap(b * PER_SLOT[0]), act.snap(b * PER_SLOT[1])]
                for h in range(H):
                    act.wait_ge(filled, at_fill + (h + 1))
                    nc.scalar.activation(KH[:, h, :], slots[h % 2][:, 0:SP], ACT.Copy).then_inc(kh_done, 1)
                def queries(t, par):
                    act.wait_ge(q_psum, at_tile + (t + 2))
                    nc.scalar.activation(QS[0:K, t % 2, par::2, :],
                                         Q[K * par:K * par + K, :].rearrange("p (i m) -> p i m", m=P),
                                         ACT.Copy).then_inc(q_hi, 1)

                queries(0, 0)
                queries(0, 1)

                def copy_scores(g):
                    n = FILL["scores", g]
                    act.wait_ge(filled, at_fill + (n + 1))
                    if g >= 2:
                        act.wait_ge(exp_done, at_step + (g - 1))
                    nc.scalar.activation(score[:, g % 2, :], slots[n % 2][:, 0:S], ACT.Copy).then_inc(free[n % 2], 1)

                def exponentials(g):
                    act.wait_ge(max_done, at_step + (g + 1))
                    if g >= 2:
                        act.wait_ge(p_normed, at_step + (g - 1))
                        act.wait_ge(rden_done, at_step + (g - 1))
                    nc.scalar.activation(prob[:, g % 2, :], score[:, g % 2, :], ACT.Exp, bias=rmax[:, g % 2:g % 2 + 1],
                                         scale=-1.0, accum_out=den[:, g % 2:g % 2 + 1]).then_inc(exp_done, 1)

                def evacuate(g):
                    act.wait_ge(p_turned, at_step + (g + 1))
                    if g >= 2:
                        act.wait_ge(pv_done, at_step + g)
                    nc.scalar.activation(pT[:, g % 2, :], PTf[:, 0:NT * P], ACT.Copy).then_inc(pt_evac, 1)

                copy_scores(0)
                copy_scores(1)
                for t in range(0, NT, 2):
                    n = FILL["values", t]
                    act.wait_ge(filled, at_fill + (n + 1))
                    nc.scalar.activation(Vt[:, t, :], slots[n % 2], ACT.Copy).then_inc(free[n % 2], 1)
                for g in range(STEPS):
                    exponentials(g)
                    if g + 2 < STEPS:
                        copy_scores(g + 2)
                    if g % 2 == 1:
                        evacuate(g - 1)
                    if g % H in QSTEPS_ACT and g // H + 1 < NT:
                        queries(g // H + 1, QSTEPS_ACT.index(g % H))

            for n in range(2):
                if n == 1:
                    act.wait_ge(x3_turned, TILES + 2)
                    nc.scalar.activation(x3T[:, :], PTf[:, NT * P:(NT + 1) * P], ACT.Copy).then_inc(x3_evac, 1)
                act.wait_ge(lg_done, TILES + 1 + n)
                nc.scalar.activation(lg_row[:, TILES + n, :], PTf[:, LG:LG + E], ACT.Copy).then_inc(lg_evac, 1)
            act.wait_ge(l_ready, 1)
            nc.scalar.activation(psel, psel, ACT.Exp).then_inc(l_exp, 1)

            def evacuate_turned(i, s):
                act.wait_ge(f_turned, i + 1)
                nc.scalar.activation(fT[:, s, :], Q[:, 0:P], ACT.Copy).then_inc(fT_ready, 1)

            def gelu(i, s):
                act.wait_ge(up_biased, i + 1)
                nc.scalar.activation(act_h[:, s, :], hid[:, s, :], ACT.Gelu).then_inc(gelu_done, 1)

            evacuate_turned(0, 0)
            evacuate_turned(1, 1)
            gelu(0, 0)
            evacuate_turned(2, 2)
            for i, s, _ in expert_tiles(act):
                if later(i, 1):
                    gelu(i + 1, (s + 1) % UN)
                if later(i, 3):
                    evacuate_turned(i + 3, (s + 3) % UN)

        @block.gpsimd
        def _(pool):
            pool.sem_inc(q_psum)
            n_step = [0]

            def settle_pool():
                pool.sem_inc(settled_pool)


            def step(ins):
                n_step[0] += 1
                ins.then_inc(pool_step, 1)
                pool.wait_ge(pool_step, n_step[0])

            step(nc.gpsimd.memset(ident[:, :], 0.0))
            step(nc.gpsimd.affine_select(out=ident[:, :], in_=ident[:, :], compare_op=ALU.not_equal, fill=1.0, base=0,
                                         pattern=[[-1, P]], channel_multiplier=1))
            nc.gpsimd.memset(half[:, :], -0.5).then_inc(consts_ready, 1)
            step(nc.gpsimd.memset(blank[:, :], 0.0))
            nc.gpsimd.memset(blank[:, TOKEN:TOKEN + 1].bitcast(I32), SKIP).then_inc(consts_ready, 1)
            step(nc.gpsimd.memset(eps2[:, 0:1], 1e-6))
            step(nc.gpsimd.memset(eps2[:, 1:2], 1e-5))
            step(nc.gpsimd.memset(ones[:, :], 1.0))
            step(nc.gpsimd.affine_select(out=before[:, :], in_=ones[:, :], compare_op=ALU.is_gt, fill=0.0, base=0,
                                         pattern=[[1, P]], channel_multiplier=-1))
            step(nc.gpsimd.iota(rampi[:, :], pattern=[[1, 32]], base=0, channel_multiplier=0))
            tid = tokid[:, :].rearrange("p (b t) -> p b t", t=NT)
            step(nc.gpsimd.iota(tid[:, :, 0:NX], pattern=[[S, B], [P, NX]], base=SEQ, channel_multiplier=1))
            step(nc.gpsimd.iota(tid[:, :, NX], pattern=[[S, B]], base=1, channel_multiplier=1))
            step(nc.gpsimd.iota(tid[NPATCH:SEQ, :, NX], pattern=[[S, B]], base=0, channel_multiplier=0))
            nc.gpsimd.memset(valid[:, :], 1.0).then_inc(pool_step, 1)
            n_step[0] += 1
            pool.wait_ge(pool_step, n_step[0])
            nc.gpsimd.affine_select(out=valid[:, NX::NT], in_=valid[:, NX::NT], compare_op=ALU.is_gt, fill=0.0,
                                    base=SEQ, pattern=[[0, B]], channel_multiplier=-1).then_inc(consts_ready, 1)
            rs = rstd[:, :].rearrange("p (b t) -> p b t", t=NT)
            vs = var[:, :].rearrange("p (b t) -> p b t", t=NT)
            hs = half[:, :].rearrange("p (b t) -> p b t", t=NT)
            for n, part in enumerate((slice(0, NX), slice(NX, NT))):
                pool.wait_ge(stat_ready, n + 1)
                nc.gpsimd.tensor_tensor(rs[:, :, part], vs[:, :, part], hs[:, :, part], ALU.pow).then_inc(rstd_ready, 1)
            pool.wait_ge(normed, 2)
            pool.wait_ge(ld_small, 160)
            nc.gpsimd.tensor_tensor(y_all, xn_all[:, :, :],
                                    boS[:, :].unsqueeze(1).to_broadcast([P, TILES, D]), ALU.add).then_inc(y_init, 1)
            nc.gpsimd.tensor_tensor(h_all, h_all, betaS[:, :].unsqueeze(1).to_broadcast([P, TILES, D]), ALU.add)\
                .then_inc(y_init, 1)
            pool.wait_ge(pre_evac, 7 + B)

            def power(n, row):
                variance = (stat, stat3)[n][:, 1:2]
                pool.wait_ge(stat_done, row * 2 + (n + 1))
                nc.gpsimd.tensor_tensor(spread[:, n:n + 1], variance, eps2[:, n:n + 1], ALU.add)\
                    .then_inc(spread_done, 1)
                pool.wait_ge(spread_done, row * 2 + (n + 1))
                nc.gpsimd.tensor_tensor(variance, spread[:, n:n + 1], half[:, 0:1], ALU.pow).then_inc(rstd3_done, 1)
                if n == 1:
                    pool.wait_ge(rstd3_done, row * 2 + 2)
                    settle_pool()
                    nc.gpsimd.tensor_copy(h_row[:, bass.ds(row, 1), MEAN:MEAN + 2].rearrange("p a c -> p (a c)"),
                                          stat3[:, :]).then_inc(stat_kept, 1)

            nc.gpsimd.tensor_copy(xs[:, :], xT_all[:, 0, :]).then_inc(xs_ready, 1)
            with pool.Fori(0, B) as b:
                at_step = pool.snap(b * STEPS)
                at_tile = pool.snap(b * NT)
                for g in range(STEPS):
                    pool.wait_ge(rden_done, at_step + (g + 1))
                    if g >= 2:
                        pool.wait_ge(p_turned, at_step + (g - 1))
                    settle_pool()
                    nc.gpsimd.tensor_scalar(pn[:, g % 2, 0:S], prob[:, g % 2, :], rden[:, g % 2:g % 2 + 1], 1.0,
                                            ALU.mult, ALU.mult).then_inc(p_normed, 1)
                    row = at_tile + g // H
                    if g % H == POW2:
                        power(0, row)
                    if g % H == POW3:
                        power(1, row)
                    if g == STEPS - 4:
                        pool.wait_ge(q_lo, (at_tile + NT) * 2 + 1)
                        nc.gpsimd.tensor_copy(xs[:, :], xT_all[:, bass.ds(b + 1, 1), :].rearrange("p a n -> p (a n)"))\
                            .then_inc(xs_ready, 1)
            power(0, TILES)
            power(1, TILES)
            pool.wait_ge(slots_ready, 1)
            pool.wait_ge(stat_kept, TILES + 2)
            pool.wait_ge(ld_blank, 16)
            for t in range(TILES):
                nc.gpsimd.indirect_dma_start(
                    out=by_expert[:, :], out_offset=bass.IndirectOffsetOnAxis(ap=slotu[:, t:t + 1], axis=0),
                    in_=h_row[:, t + 1, :], in_offset=None, bounds_check=SORTED * P - 1, oob_is_err=False)\
                    .then_inc(rows_out, 16)
            for i, s, _ in expert_tiles(pool):
                pool.wait_ge(yo_ready, i + 1)
                settle_pool()
                nc.gpsimd.indirect_dma_start(
                    out=out_rows, out_offset=bass.IndirectOffsetOnAxis(ap=idx[:, s:s + 1], axis=0),
                    in_=yo[:, s, :], in_offset=None, bounds_check=TOKENS - 1, oob_is_err=False)\
                    .then_inc(out_done[s], 16)
            for s in range(UN):
                pool.wait_ge(out_done[s], 16 * len(range(s, SORTED, UN)))

        @block.vector
        def _(dve):
            dve.sem_inc(pv_done)
            dve.sem_inc(x3_turned)
            dve.sem_inc(stat_kept)
            n_step = [0]

            def settle_vec():
                dve.sem_inc(settled_vec)


            def step(ins):
                n_step[0] += 1
                ins.then_inc(vec_step, 1)
                dve.wait_ge(vec_step, n_step[0])

            h_v = h_all.rearrange("p (b t) d -> p b t d", t=NT)
            xn_v = xn_all[:, :, :].rearrange("p (b t) d -> p b t d", t=NT)
            sq_v = xT_all[:, 0:B, :].rearrange("p b (t d) -> p b t d", t=NT)
            mean_v = mean[:, :].rearrange("p (b t) -> p b t", t=NT)
            var_v = var[:, :].rearrange("p (b t) -> p b t", t=NT)
            rstd_v = rstd[:, :].rearrange("p (b t) -> p b t", t=NT)

            def wide(a, like):
                return a.unsqueeze(len(a.shape)).to_broadcast(list(like.shape))

            def normalise(n, src, cen, sq, m, v, r, eps, last=None):
                step(nc.vector.tensor_reduce(m, src, AX.X, ALU.add))
                step(nc.vector.tensor_scalar(m, m, 1.0 / D, None, ALU.mult))
                nc.vector.tensor_tensor(cen, src, wide(m, src), ALU.subtract).then_inc(centred, 1)
                dve.wait_ge(squared, n)
                step(nc.vector.tensor_reduce(v, sq, AX.X, ALU.add))
                nc.vector.tensor_scalar(v, v, 1.0 / D, eps, ALU.mult, ALU.add).then_inc(stat_ready, 1)
                dve.wait_ge(rstd_ready, n)
                nc.vector.tensor_tensor(cen, cen, wide(r, src), ALU.mult).then_inc(normed, 1)
                dve.wait_ge(normed, n)

            step(nc.vector.memset(h_v[NPATCH:P, :, NX, :], 0.0))
            step(nc.vector.memset(PTf[:, NX * P:NT * P], 0.0))
            step(nc.vector.memset(h_row[:, 0, :], 0.0))
            step(nc.vector.memset(y_row[:, 0, :], 0.0))
            step(nc.vector.memset(x3T[:, :], 0.0))
            step(nc.vector.memset(xT_all[:, B, :], 0.0))
            step(nc.vector.memset(pn[:, :, S:NT * P], 0.0))
            dve.wait_ge(ld_txt, 16 * B)
            normalise(1, h_v[:, :, 0:NX, :], xn_v[:, :, 0:NX, :], sq_v[:, :, 0:NX, :],
                      mean_v[:, :, 0:NX], var_v[:, :, 0:NX], rstd_v[:, :, 0:NX], 1e-5)
            dve.wait_ge(ld_small, 160)
            step(nc.vector.tensor_tensor(h_v[NPATCH:SEQ, :, NX, :],
                                         clsS[NPATCH:SEQ, :].unsqueeze(1).to_broadcast([1, B, D]),
                                         posS[NPATCH:SEQ, :].unsqueeze(1).to_broadcast([1, B, D]), ALU.mult))
            dve.wait_ge(pre_fill, 8)
            step(nc.vector.tensor_tensor(h_v[0:NPATCH, :, NX, :],
                                         O[0:NPATCH, :].rearrange("p (b d) -> p b d", b=B),
                                         posS[0:NPATCH, :].unsqueeze(1).to_broadcast([NPATCH, B, D]), ALU.mult))
            step(nc.vector.memset(O[:, 0:D], 0.0))
            normalise(2, h_v[:, :, NX, :], xn_v[:, :, NX, :], sq_v[:, :, NX, :],
                      mean_v[:, :, NX], var_v[:, :, NX], rstd_v[:, :, NX], 1e-5)

            dve.wait_ge(y_init, 2)

            def tile_row(row, c, n):
                return h_row[:, bass.ds(row, 1), c:c + n].rearrange("p a d -> p (a d)")

            def attention_residual(row, steps):
                dve.wait_ge(pv_done, steps + 1)
                y = y_row[:, bass.ds(row, 1), :].rearrange("p a d -> p (a d)")
                nc.vector.tensor_tensor(y, O[:, 0:D], y, ALU.add).then_inc(y_done, 1)

            def statistics(row, n):
                if n == 0:
                    dve.wait_ge(y_done, row + 1)
                    src = y_row[:, bass.ds(row, 1), :].rearrange("p a d -> p (a d)")
                else:
                    dve.wait_ge(h_done, row + 1)
                    dve.wait_ge(stat_kept, row + 1)
                    src = tile_row(row, 0, D)
                settle_vec()
                nc.vector.bn_stats(six[:, :], src).then_inc(six_done, 1)
                dve.wait_ge(six_done, row * 2 + (n + 1))
                settle_vec()
                nc.vector.bn_aggr((stat, stat3)[n][:, :], six[:, :]).then_inc(stat_done, 1)

            def normalised_residual(row):
                dve.wait_ge(rstd3_done, row * 2 + 1)
                y = y_row[:, bass.ds(row, 1), :].rearrange("p a d -> p (a d)")
                nc.vector.scalar_tensor_tensor(out=scaled[:, :], in0=y, scalar=stat[:, 0:1], in1=gammaS[:, :],
                                               op0=ALU.subtract, op1=ALU.mult).then_inc(scaled_done, 1)
                dve.wait_ge(scaled_done, row + 1)
                h = tile_row(row, 0, D)
                nc.vector.scalar_tensor_tensor(out=h, in0=scaled[:, :], scalar=stat[:, 1:2], in1=h,
                                               op0=ALU.mult, op1=ALU.add).then_inc(h_done, 1)

            def third_normalisation(row):
                dve.wait_ge(rstd3_done, row * 2 + 2)
                dve.wait_ge(x3_turned, row + 1)
                nc.vector.tensor_scalar(x3[:, :], tile_row(row, 0, D), stat3[:, 0:1], stat3[:, 1:2],
                                        ALU.subtract, ALU.mult).then_inc(x3_done, 1)

            with dve.Fori(0, B) as b:
                at_fill = dve.snap(b * FILLS)
                at_step = dve.snap(b * STEPS)
                at_tile = dve.snap(b * NT)
                at_head = dve.snap(b * H)
                at_slot = [dve.snap(b * PER_SLOT[0]), dve.snap(b * PER_SLOT[1])]
                for h in range(H):
                    dve.wait_ge(kh_done, at_head + (h + 1))
                    nc.vector.tensor_tensor(KL[:, h, :], slots[h % 2][:, 0:SP], KH[:, h, :].bitcast(F32), ALU.subtract)\
                        .then_inc(free[h % 2], 1)
                def queries(t, par):
                    dve.wait_ge(q_hi, (at_tile + t) * 2 + (par + 1))
                    nc.vector.tensor_tensor(QS[K:2 * K, t % 2, par::2, :],
                                            Q[K * par:K * par + K, :].rearrange("p (i m) -> p i m", m=P),
                                            QS[0:K, t % 2, par::2, :].bitcast(F32), ALU.subtract).then_inc(q_lo, 1)

                queries(0, 0)
                queries(0, 1)

                def reciprocals(g):
                    dve.wait_ge(exp_done, at_step + (g + 1))
                    if g >= 2:
                        dve.wait_ge(p_normed, at_step + (g - 1))
                    nc.vector.reciprocal(rden[:, g % 2:g % 2 + 1], den[:, g % 2:g % 2 + 1]).then_inc(rden_done, 1)

                def mask_and_max(g):
                    n = FILL["scores", g]
                    dve.wait_ge(free[n % 2], at_slot[n % 2] + (n // 2 + 2))
                    if g >= 1:
                        dve.wait_ge(max_done, at_step + g)
                    nc.vector.tensor_scalar(zero_mark[:, :], score[:, g % 2, :], 0.0, -1e9 * K ** 0.5,
                                            ALU.is_equal, ALU.mult).then_inc(z_done, 1)
                    dve.wait_ge(z_done, at_step + (g + 1))
                    settle_vec()
                    nc.vector.tensor_tensor_reduce(score[:, g % 2, :], score[:, g % 2, :], zero_mark[:, :],
                                                   -(K ** -0.5), 3e38, ALU.add, ALU.min,
                                                   rmax[:, g % 2:g % 2 + 1]).then_inc(max_done, 1)

                def evacuate(g):
                    dve.wait_ge(p_turned, at_step + (g + 1))
                    if g >= 2:
                        dve.wait_ge(pv_done, at_step + g)
                    if g % H == 7:
                        nc.vector.tensor_copy(x3T[:, :], PTf[:, NT * P:(NT + 1) * P]).then_inc(x3_evac, 1)
                    if g % H == 1:
                        nc.vector.tensor_copy(lg_row[:, bass.ds(at_tile + g // H, 1), :].rearrange("p a e -> p (a e)"),
                                              PTf[:, LG:LG + E]).then_inc(lg_evac, 1)
                    nc.vector.tensor_copy(pT[:, g % 2, :], PTf[:, 0:NT * P]).then_inc(pt_evac, 1)

                mask_and_max(0)
                for t in range(1, NT, 2):
                    n = FILL["values", t]
                    dve.wait_ge(filled, at_fill + (n + 1))
                    nc.vector.tensor_copy(Vt[:, t, :], slots[n % 2]).then_inc(free[n % 2], 1)
                for g in range(STEPS):
                    if g + 1 < STEPS:
                        mask_and_max(g + 1)
                    reciprocals(g)
                    row = at_tile + g // H
                    if g % H == 2:
                        attention_residual(row, at_step + g // H * H)
                    if g >= 1 and (g - 1) % 2 == 1:
                        evacuate(g - 1)
                    if g % H in QSTEPS_VEC and g // H + 1 < NT:
                        queries(g // H + 1, QSTEPS_VEC.index(g % H))
                    if g % H == 4:
                        statistics(row, 0)
                    if g % H == 5:
                        normalised_residual(row)
                    if g % H == 6:
                        statistics(row, 1)
                    if g % H == 7:
                        third_normalisation(row)
                evacuate(STEPS - 1)

            attention_residual(TILES, B * STEPS)
            statistics(TILES, 0)
            normalised_residual(TILES)
            statistics(TILES, 1)
            third_normalisation(TILES)

            dve.wait_ge(consts_ready, 3)
            step(nc.vector.tensor_copy(ramp[:, :], rampi[:, :]))
            step(nc.vector.tensor_scalar(rampP[:, :], ramp[:, :], float(P), None, ALU.mult))
            step(nc.vector.tensor_scalar(order[:, :], ramp[:, 0:E], -1.0, float(E), ALU.mult, ALU.add))
            step(nc.vector.memset(fresh[:, :, :], 1.0))
            step(nc.vector.memset(fresh[:, :, 0:1], 0.0))
            step(nc.vector.memset(one8[:, :], 1.0))

            dve.wait_ge(lg_evac, TILES + 2)
            lg = lg_row[:, 2:, :]
            step(nc.vector.tensor_tensor(logit[:, :, :], lg, bsS[:, :].unsqueeze(1).to_broadcast([P, TILES, E]), ALU.add))
            step(nc.vector.tensor_reduce(lmax[:, :], logit[:, :, :], AX.X, ALU.max))
            nc.vector.tensor_tensor(psel[:, :, :], logit[:, :, :], wide(lmax[:, :], logit[:, :, :]), ALU.subtract)\
                .then_inc(l_ready, 1)
            hot_t = hot[:, :, :].rearrange("p e t -> p t e")
            step(nc.vector.tensor_tensor(hot_t, logit[:, :, :], wide(lmax[:, :], logit[:, :, :]), ALU.is_equal))
            step(nc.vector.tensor_tensor(hot_t, hot_t, order[:, :].unsqueeze(1).to_broadcast([P, TILES, E]), ALU.mult))
            step(nc.vector.tensor_reduce(slotf[:, :], hot_t, AX.X, ALU.max))
            step(nc.vector.tensor_tensor(hot_t, order[:, :].unsqueeze(1).to_broadcast([P, TILES, E]),
                                         wide(slotf[:, :], logit[:, :, :]), ALU.is_equal))
            nc.vector.tensor_tensor(hot_t, hot_t, wide(valid[:, :], logit[:, :, :]), ALU.mult).then_inc(hot_ready, 1)
            dve.wait_ge(l_exp, 1)
            step(nc.vector.tensor_reduce(psum_[:, :], psel[:, :, :], AX.X, ALU.add))
            step(nc.vector.reciprocal(pbest[:, :], psum_[:, :]))
            step(nc.vector.tensor_copy(h_row[:, 1:, PBEST], pbest[:, :]))
            step(nc.vector.tensor_copy(h_row[:, 1:, TOKEN].bitcast(I32), tokid[:, :]))

            dve.wait_ge(ranks_done, 1)
            rank = O[:, 0:E * TILES].rearrange("p (e t) -> p e t", e=E)
            count = Q[:, 0:E * TILES]
            flat = "p e t -> p (e t)"
            step(nc.vector.tensor_tensor_scan(incl[:, :, :].rearrange(flat), fresh[:, :, :].rearrange(flat), count, 0.0,
                                              ALU.mult, ALU.add))
            step(nc.vector.tensor_tensor(base[:, :, :].rearrange(flat), incl[:, :, :].rearrange(flat), count,
                                         ALU.subtract))
            cm = cmp[:, 0:E * TILES].rearrange("p (e t) -> p e t", e=E)
            step(nc.vector.tensor_tensor(cm, incl[:, :, TILES - 1:TILES].to_broadcast([P, E, TILES]),
                                         rampP[:, 0:TILES].unsqueeze(1).to_broadcast([P, E, TILES]), ALU.is_gt))
            step(nc.vector.tensor_reduce(ntile[:, :], cm, AX.X, ALU.add))
            step(nc.vector.tensor_tensor_scan(tend[:, :], one8[:, :], ntile[:, :], 0.0, ALU.mult, ALU.add))
            ce = cmp[:, 0:SORTED * E].rearrange("p (i e) -> p i e", e=E)
            step(nc.vector.tensor_tensor(ce, wide(ramp[:, 0:SORTED], ce),
                                         tend[:, :].unsqueeze(1).to_broadcast([P, SORTED, E]), ALU.is_ge))
            step(nc.vector.tensor_reduce(exf[:, :], ce, AX.X, ALU.add))
            step(nc.vector.tensor_scalar(exf[:, :], exf[:, :], float(E - 1), None, ALU.min))
            nc.vector.tensor_copy(exi[:, :], exf[:, :]).then_inc(experts_ready, 1)
            step(nc.vector.tensor_tensor(tend[:, :], tend[:, :], ntile[:, :], ALU.subtract))
            step(nc.vector.tensor_scalar(tend[:, :], tend[:, :], float(P), None, ALU.mult))
            step(nc.vector.tensor_tensor(base[:, :, :], base[:, :, :], wide(tend[:, :], base[:, :, :]), ALU.add))
            step(nc.vector.tensor_tensor(base[:, :, :], rank, base[:, :, :], ALU.add))
            step(nc.vector.tensor_tensor(base[:, :, :], base[:, :, :], hot[:, :, :], ALU.mult))
            step(nc.vector.tensor_reduce(slotf[:, :], base[:, :, :].rearrange("p e t -> p t e"), AX.X, ALU.add))
            step(nc.vector.tensor_scalar(lmax[:, :], valid[:, :], -float(SKIP), float(SKIP), ALU.mult, ALU.add))
            step(nc.vector.tensor_tensor(slotf[:, :], slotf[:, :], lmax[:, :], ALU.add))
            nc.vector.tensor_copy(slotu[:, :], slotf[:, :]).then_inc(slots_ready, 1)

            dve.wait_ge(experts_ready, 1)
            dve.wait_ge(ld_experts, 48)
            dve.wait_ge(rows_in, 16 * (SORTED // 5))

            def row_of(i, c, n):
                return sorted_in[:, bass.ds(i, 1), c:c + n].rearrange("p a c -> p (a c)")

            def expert(i):
                return dve.value_load(exi[0:1, bass.ds(i, 1)], min_val=0, max_val=E - 1)

            def normalise_rows(i, s):
                nc.vector.tensor_scalar(xf[:, s, :], row_of(i, 0, D), row_of(i, MEAN, 1), row_of(i, RSTD, 1),
                                        ALU.subtract, ALU.mult).then_inc(xf_ready, 1)

            def up(i, s):
                e = expert(i)
                dve.wait_ge(up_done, i + 1)
                nc.vector.tensor_tensor(hid[:, s, :], SL[:, s, :], b1S[:, bass.ds(e * FF, FF)], ALU.add)\
                    .then_inc(up_biased, 1)

            def turned(i, s):
                dve.wait_ge(hid_turned, i + 1)
                nc.vector.tensor_copy(hidT[:, s, :], hidT_ps[s]).then_inc(hidT_ready, 1)

            def down(i, s, turns):
                e = expert(i)
                dve.wait_ge(down_done, i + 1)
                if not isinstance(turns, int) or turns > 0:
                    dve.wait_ge(out_done[s], turns * 16)
                nc.vector.tensor_tensor(yo[:, s, :], O[:, 0:D], b2S[:, bass.ds(e * D, D)], ALU.add).then_inc(yb_done, 1)
                nc.vector.tensor_copy(idx[:, s:s + 1], row_of(i, TOKEN, 1).bitcast(U32)).then_inc(yb_done, 1)
                dve.wait_ge(yb_done, i * 2 + 2)
                nc.vector.scalar_tensor_tensor(out=yo[:, s, :], in0=yo[:, s, :], scalar=row_of(i, PBEST, 1),
                                               in1=row_of(i, 0, D), op0=ALU.mult, op1=ALU.add).then_inc(yo_ready, 1)

            normalise_rows(0, 0)
            normalise_rows(1, 1)
            normalise_rows(2, 2)
            up(0, 0)
            dve.wait_ge(f_turned, 1)
            normalise_rows(3, 0)
            for i, s, turns in expert_tiles(dve):
                if later(i, 1):
                    up(i + 1, (s + 1) % UN)
                turned(i, s)
                if not isinstance(i, int) or i > 0:
                    down(i - 1, (s - 1) % UN, turns if s > 0 else turns - 1)
                if later(i, AHEAD):
                    normalise_rows(i + AHEAD, (s + AHEAD) % UN)
            down(SORTED - 1, (SORTED - 1) % UN, (SORTED - 1) // UN)

        @block.tensor
        def _(pe):
            for primed in (*free, q_lo, x3_evac):
                pe.sem_inc(primed)
            pe.wait_ge(consts_ready, 1)
            pe.wait_ge(ld_attn, 16 * 5)
            for h in range(H):
                last = nc.tensor.transpose(slots[0][:, h * D:(h + 1) * D], WvS[:, h * D:(h + 1) * D], ident[:, :])
            last.then_inc(pre_fill, 1)
            pe.wait_ge(pre_evac, 1)
            for h in range(H):
                last = nc.tensor.matmul(slots[1][:, h * D:(h + 1) * D], WvT[:, h * D:(h + 1) * D], WoS[:, h, :],
                                        start=True, stop=True)
            last.then_inc(pre_fill, 1)
            pe.wait_ge(ld_tok, 16 * (1 + B * C))
            for g in range(4):
                n = min(8, PX - 8 * g)
                pe.wait_ge(pre_evac, g + 1)
                for j in range(n):
                    last = nc.tensor.transpose(slots[g % 2][0:CI, j * D:(j + 1) * D], WtS[:, 8 * g + j::PX], ident[:, :])
                last.then_inc(pre_fill, 1)
            pe.wait_ge(pre_evac, 6)
            Xv = X.rearrange("p g (w j) -> p g w j", j=PX)
            for j in range(PX):
                last = nc.tensor.matmul(Q[:, 0:B * NPATCH].rearrange("p (g w) -> p g w", w=GRID), WtT[:, j, :], Xv[:, :, :, j],
                                        start=(j == 0), stop=(j == PX - 1))
            last.then_inc(pre_fill, 1)
            pe.wait_ge(pre_evac, 7)
            for b in range(B):
                last = nc.tensor.transpose(O[0:NPATCH, b * D:(b + 1) * D], tokT[:, b * NPATCH:(b + 1) * NPATCH],
                                           ident[:, :])
            last.then_inc(pre_fill, 1)
            pe.wait_ge(normed, 2)
            for b in range(B):
                if b >= 2:
                    pe.wait_ge(pre_evac, 6 + b)
                for t in range(NT):
                    last = nc.tensor.transpose(slots[b % 2][:, t * P:(t + 1) * P], xn_all[:, b * NT + t, :], ident[:, :])
                last.then_inc(pre_fill, 1)

            pe.wait_ge(pre_evac, 7 + B)

            def turn_tile(row):
                pe.wait_ge(x3_done, row + 1)
                nc.tensor.transpose(PTf[:, NT * P:(NT + 1) * P], x3[:, :], ident[:, :]).then_inc(x3_turned, 1)

            def route_tile(row):
                pe.wait_ge(x3_evac, row + 1)
                nc.tensor.matmul(PTf[:, LG:LG + E], x3T[:, :], WsS[:, :], start=True, stop=True).then_inc(lg_done, 1)

            with pe.Fori(0, B) as b:
                at_step = pe.snap(b * STEPS)
                at_tile = pe.snap(b * NT)
                at_slot = [pe.snap(b * PER_SLOT[0]), pe.snap(b * PER_SLOT[1])]

                def wait_slot(n):
                    pe.wait_ge(free[n % 2], at_slot[n % 2] + (n // 2 + 1))

                def queries(t):
                    pe.wait_ge(q_lo, (at_tile + t) * 2 + 1)
                    for i in range(H // 2):
                        last = nc.tensor.matmul(Q[:, i * P:(i + 1) * P], WqS[:, i * P:(i + 1) * P],
                                                xs[:, t * P:(t + 1) * P], start=True, stop=True)
                    last.then_inc(q_psum, 1)

                def scores(g):
                    t, h = divmod(g, H)
                    n = FILL["scores", g]
                    wait_slot(n)
                    if h == 0:
                        pe.wait_ge(q_lo, (at_tile + t) * 2 + 3)
                    for a, c in ((0, 512), (512, SP)):
                        for part, keys in enumerate((KH, KL)):
                            last = nc.tensor.matmul(slots[n % 2][:, a:c], QS[:, t % 2, h, :], keys[:, h, a:c],
                                                    start=(part == 0), stop=(part == 1))
                    last.then_inc(filled, 1)

                def turn(g):
                    pe.wait_ge(p_normed, at_step + (g + 1))
                    if g >= 1:
                        pe.wait_ge(pt_evac, at_step + g)
                    if g % H == 7:
                        turn_tile(at_tile + g // H)
                    if g % H == 1:
                        route_tile(at_tile + g // H)
                    for t in range(NT):
                        n = P if t < NX else TAIL
                        last = nc.tensor.transpose(PTf[0:n, t * P:(t + 1) * P], pn[:, g % 2, t * P:t * P + n], ident[:, :])
                    last.then_inc(p_turned, 1)

                def values(g):
                    tile, h = divmod(g, H)
                    pe.wait_ge(pt_evac, at_step + (g + 1))
                    if h == 0:
                        pe.wait_ge(y_done, at_tile + (tile + 1))
                    for t in range(NT):
                        n = P if t < NX else TAIL
                        last = nc.tensor.matmul(O[:, 0:D], pT[0:n, g % 2, t * P:(t + 1) * P],
                                                Vt[0:n, t, h * D:(h + 1) * D],
                                                start=(h == 0 and t == 0), stop=(h == H - 1 and t == NX))
                    last.then_inc(pv_done, 1)

                pe.wait_ge(xs_ready, b + 1)
                for h in range(H):
                    wait_slot(h)
                    for a, c in ((0, 512), (512, SP)):
                        last = nc.tensor.matmul(slots[h % 2][:, a:c], WkS[:, h, :, :].rearrange("p a k -> p (a k)"), xs[:, a:c],
                                                start=True, stop=True)
                    last.then_inc(filled, 1)
                queries(0)
                scores(0)
                scores(1)
                for t in range(NT):
                    n = FILL["values", t]
                    wait_slot(n)
                    for c in range(2):
                        last = nc.tensor.matmul(slots[n % 2][:, c * 512:(c + 1) * 512], xs[:, t * P:(t + 1) * P],
                                                VO[:, c * 512:(c + 1) * 512], start=True, stop=True)
                    last.then_inc(filled, 1)
                for g in range(2, LEAD):
                    scores(g)
                for g in range(STEPS):
                    if g % H == QSTEP and g // H + 1 < NT:
                        queries(g // H + 1)
                    if g + LEAD < STEPS:
                        scores(g + LEAD)
                    if g >= 1:
                        turn(g - 1)
                    if g >= 2:
                        values(g - 2)
                turn(STEPS - 1)
                values(STEPS - 2)
                values(STEPS - 1)

            pe.wait_ge(pt_evac, B * STEPS)
            route_tile(TILES)
            pe.wait_ge(lg_evac, TILES + 1)
            turn_tile(TILES)
            route_tile(TILES + 1)
            pe.wait_ge(hot_ready, 1)
            flat_hot = hot[:, :, :].rearrange("p e t -> p (e t)")
            nc.tensor.matmul(O[:, 0:E * TILES], before[:, :], flat_hot, start=True, stop=True)
            nc.tensor.matmul(Q[:, 0:E * TILES], ones[:, :], flat_hot, start=True, stop=True).then_inc(ranks_done, 1)

            pe.wait_ge(experts_ready, 1)
            pe.wait_ge(slots_ready, 1)
            pe.wait_ge(ld_experts, 48)

            def expert(i):
                return pe.value_load(exi[0:1, bass.ds(i, 1)], min_val=0, max_val=E - 1)

            def turn_rows(i, s):
                pe.wait_ge(xf_ready, i + 1)
                nc.tensor.transpose(Q[:, 0:P], xf[:, s, :], ident[:, :]).then_inc(f_turned, 1)

            def up(i, s):
                e = expert(i)
                pe.wait_ge(fT_ready, i + 1)
                nc.tensor.matmul(SL[:, s, :], fT[:, s, :], W1S[:, bass.ds(e * FF, FF)], start=True, stop=True)\
                    .then_inc(up_done, 1)

            def turn_hidden(i, s):
                pe.wait_ge(gelu_done, i + 1)
                for c in range(NF):
                    last = nc.tensor.transpose(hidT_ps[s][:, c * P:(c + 1) * P], act_h[:, s, c * P:(c + 1) * P],
                                               ident[:, :])
                last.then_inc(hid_turned, 1)

            def down(i, s):
                e = expert(i)
                pe.wait_ge(hidT_ready, i + 1)
                if not isinstance(i, int) or i > 0:
                    pe.wait_ge(yb_done, i * 2)
                for c in range(NF):
                    last = nc.tensor.matmul(O[:, 0:D], hidT[:, s, c * P:(c + 1) * P],
                                            W2S[:, bass.ds(e * (NF * D) + c * D, D)],
                                            start=(c == 0), stop=(c == NF - 1))
                last.then_inc(down_done, 1)

            turn_rows(0, 0)
            up(0, 0)
            turn_rows(1, 1)
            up(1, 1)
            turn_rows(2, 2)
            for i, s, _ in expert_tiles(pe):
                turn_hidden(i, s)
                if not isinstance(i, int) or i > 0:
                    down(i - 1, (s - 1) % UN)
                if later(i, 2):
                    up(i + 2, (s + 2) % UN)
                if later(i, 3):
                    turn_rows(i + 3, (s + 3) % UN)
            down(SORTED - 1, (SORTED - 1) % UN)


LEAD, QSTEP = 3, 0
QSTEPS_ACT, QSTEPS_VEC = (0, 2), (1, 3)
POW2, POW3 = 4, 6

_INS = ['x', 'txt', 'L0_tok_W', 'L0_tok_b', 'L0_tok_class_token', 'L0_tok_pos_embed', 'L0_attn_Wq', 'L0_attn_Wk',
        'L0_attn_Wv', 'L0_attn_Wo', 'L0_attn_bo', 'L0_attn_gamma', 'L0_attn_beta', 'L0_ffn_Ws', 'L0_ffn_bs',
        'L0_ffn_W1', 'L0_ffn_b1', 'L0_ffn_W2', 'L0_ffn_b2']


def kernel(**inputs):
    import numpy as _np
    import concourse.bacc as _bacc
    from concourse import mybir as _mybir
    from concourse.bass_utils import run_bass_kernel_spmd as _run

    nc = _bacc.Bacc("TRN2", target_bir_lowering=False, num_devices=1)
    arrays, args = {}, []
    for name in _INS:
        a = _np.ascontiguousarray(inputs[name])
        arrays[f"in_{name}_dram"] = a
        args.append(nc.dram_tensor(f"in_{name}_dram", a.shape, _mybir.dt.from_np(a.dtype), kind="ExternalInput").ap())
    B, C, IMG, _ = inputs['x'].shape
    NTXT, D = inputs['txt'].shape[1:]
    S = inputs['L0_tok_pos_embed'].shape[0] + NTXT
    E = inputs['L0_ffn_Ws'].shape[1]
    out = nc.dram_tensor("out_0_dram", (B, S, D), _mybir.dt.float32, kind="ExternalOutput").ap()
    n_sorted = ((B * S - E) // 128 + E) * 128
    by_expert = nc.dram_tensor("rows_by_expert", (n_sorted, D + 4), _mybir.dt.float32, kind="Internal").ap()
    early_fusion_kernel(nc, *args, out, by_expert)
    r = _run(nc, [arrays], core_ids=[0])
    return r.results[0]["out_0_dram"]
```

```python
from contextlib import ExitStack

import concourse.bass as bass
from concourse import mybir

F32 = mybir.dt.float32
F32R = mybir.dt.float32r
I32 = mybir.dt.int32
U32 = mybir.dt.uint32
ALU = mybir.AluOpType
ACT = mybir.ActivationFunctionType
AX = mybir.AxisListType

P = 128


def early_fusion_kernel(
    nc, x, txt, tok_W, tok_b, cls_tok, pos, Wq, Wk, Wv, Wo, bo, gamma, beta, Ws, bs, W1, b1, W2, b2, out, by_expert,
):
    B, C, IMG, _ = x.shape
    D = txt.shape[2]
    NTXT = txt.shape[1]
    SEQ = pos.shape[0]
    NPATCH = SEQ - 1
    GRID = int(round(NPATCH ** 0.5))
    PX = IMG // GRID
    CI = C * PX
    S = SEQ + NTXT
    K = 64
    H = Wq.shape[1] // K
    NX = NTXT // P
    NT = NX + 1
    TILES = B * NT
    SP = S + 1
    TAIL = SEQ
    FIRST = SP // 4 * 2 + 2 * (SP // 2 % 2)
    AT = 512 - FIRST
    assert AT + SP <= 1024 and FIRST <= 512
    E = Ws.shape[1]
    FF = W1.shape[2]
    NF = FF // P
    TOKENS = B * S
    REGION = -(-TOKENS // P) * P
    BLANK = E * REGION
    SORTED = (TOKENS - E) // P + E
    MEAN, RSTD, PBEST, TOKEN = range(D, D + 4)
    ROW = D + 4
    SKIP = 1 << 20
    UN = 3
    AHEAD = 4
    LOOPED = (SORTED - AHEAD) // UN
    assert D == P and NX * P == NTXT and SEQ <= P and H * K == 4 * P

    STEPS = NT * H
    fills = [("keys", pair) for pair in range(H // 2)]
    fills += [("values", 0), ("values", 1), ("scores", 0), ("scores", 1), ("values", 2), ("scores", 2), ("values", 3),
              ("values", 4)]
    fills += [("scores", g) for g in range(3, STEPS)]
    FILLS, NSLOTS = len(fills), 3
    FILL, PER_SLOT = {}, [0] * NSLOTS
    for n, fill in enumerate(fills):
        slot = n % 3 if fill[0] == "keys" else (n + 1) % 2
        FILL[fill] = (n, slot, PER_SLOT[slot])
        PER_SLOT[slot] += 1

    with ExitStack() as ctx:
        def sb(name, shape, dt=F32):
            return ctx.enter_context(nc.sbuf_tensor(name, shape, dt))

        def psum(name, shape):
            return ctx.enter_context(nc.psum_tensor(name, shape, F32))

        def sem(name):
            return ctx.enter_context(nc.semaphore(name))

        ident = sb("ident", [P, P])
        ones_r = sb("ones_r", [P, P], F32R)
        before_r = sb("before_r", [P, P], F32R)
        h_row = sb("h_row", [P, TILES + 2, ROW])
        h_all = h_row[:, 2:, 0:D]
        row_stage = sb("row_stage", [P, NT, ROW])
        y_row = sb("y_row", [P, TILES + 1, D])
        y_all = y_row[:, 1:, :]
        xn_all = sb("xn_all", [P, TILES, D])
        xT_all = sb("xT_all", [P, B, NT * P])
        xs = sb("xs", [P, NT * P])
        WqS = sb("WqS", [P, H * K])
        WkS = sb("WkS", [P, H * K])
        VO = sb("VO", [P, H * D])
        KHL = sb("KHL", [P, H, SP], F32R)
        QS = sb("QS", [P, 2, H, P], F32R)
        QX = sb("QX", [P, 2, H, P], F32R)
        V = sb("V", [P, NT * H * D])
        Vt = V[:, :].rearrange("p (t n) -> p t n", t=NT)
        WvT = V[:, 0:H * D]
        WvS = V[:, H * D:2 * H * D]
        WoS = V[:, 2 * H * D:3 * H * D].rearrange("p (h d) -> p h d", h=H)
        score = sb("score", [P, 2, S])
        zero_mark = sb("zero_mark", [P, S])
        rmax = sb("rmax", [P, 2])
        prob = sb("prob", [P, 2, S])
        ones, before = prob[:, 0, 0:P], prob[:, 0, P:2 * P]
        den = sb("den", [P, 2])
        rden = sb("rden", [P, 2])
        pn = sb("pn", [P, 2, NT * P])
        pT = sb("pT", [P, 2, NT * P])
        stage = sb("stage", [P, max(B * GRID * IMG + C * PX * PX + PX * D, E * (2 * FF + NF + D) + P)])
        X = stage[0:CI, 0:B * GRID * IMG].rearrange("p (g w) -> p g w", w=IMG)
        at = B * GRID * IMG
        WtS = stage[:, at:at + C * PX * PX]
        at += C * PX * PX
        WtT = stage[0:CI, at:at + PX * D].rearrange("p (j d) -> p j d", d=D)
        WB = FF + NF + D
        W1S = stage[:, 0:E * WB]
        W2S = stage[:, E * WB:E * (WB + FF)]
        b1S = stage[0:E * NF, E * (WB + FF):E * (WB + FF) + P]
        tokT = sb("tokT", [P, B * NPATCH])
        posS = sb("posS", [P, D])
        clsS = sb("clsS", [P, D])
        boS = sb("boS", [P, D])
        gammaS = sb("gammaS", [P, D])
        betaS = sb("betaS", [P, D])
        tbS = sb("tbS", [P, 1])
        WsS = sb("WsS", [P, E])
        bsS = sb("bsS", [P, E])
        mean = sb("mean", [P, TILES])
        var = sb("var", [P, TILES])
        rstd = sb("rstd", [P, TILES])
        half = sb("half", [P, TILES])
        minus_one = sb("minus_one", [P, 1])
        eps2 = sb("eps2", [P, 2])
        six = sb("six", [P, 6])
        stat = sb("stat", [P, 2])
        stat3 = sb("stat3", [P, 2])
        spread = sb("spread", [P, 2])
        scaled = sb("scaled", [P, D])
        x3 = sb("x3", [P, D])
        x3T = sb("x3T", [P, D])
        neg_lg = sb("neg_lg", [P, E])
        neg_max = sb("neg_max", [P, 1])
        lg_exp = sb("lg_exp", [P, E])
        lg_den = sb("lg_den", [P, 1])
        largest = sb("largest", [P, E])
        best = sb("best", [P, 1])
        hot = sb("hot", [P, E], F32R)
        ranks = sb("ranks", [P, 2 * E])
        place = sb("place", [P, E])
        slotf = sb("slotf", [P, 1])
        slot_or_skip = sb("slot_or_skip", [P, 1])
        slotu = sb("slotu", [P, NT], U32)
        running = sb("running", [P, E])
        region = sb("region", [P, E])
        valid = sb("valid", [P, TILES + 2])
        skip = sb("skip", [P, TILES + 2])
        idx = sb("idx", [P, UN], U32)
        tokid = sb("tokid", [P, TILES], I32)
        order = sb("order", [P, E])
        ramp = sb("ramp", [P, 32])
        rampi = sb("rampi", [P, 32], I32)
        rampP = sb("rampP", [P, 32])
        beyond = sb("beyond", [P, 32])
        ntile = sb("ntile", [P, E])
        tend = sb("tend", [P, E])
        tstart = sb("tstart", [P, E])
        one8 = sb("one8", [P, E])
        spare = prob[:, :, :].rearrange("p a n -> p (a n)")
        full = spare[:, 0:E * TILES].rearrange("p (e t) -> p e t", e=E)
        ended, within = (spare[:, E * TILES + n * SORTED * E:E * TILES + (n + 1) * SORTED * E]
                         .rearrange("p (i e) -> p i e", e=E) for n in range(2))
        exf = sb("exf", [P, SORTED])
        exi = sb("exi", [P, SORTED], I32)
        basef = sb("basef", [P, SORTED])
        basei = sb("basei", [P, SORTED], I32)
        blank = sb("blank", [P, ROW])
        sorted_in = V[:, 0:SORTED * ROW].rearrange("p (i c) -> p i c", c=ROW)
        at = SORTED * ROW
        hidT = V[:, at:at + UN * FF].rearrange("p (s f) -> p s f", s=UN)
        y_flat = y_row[:, :, :].rearrange("p t d -> p (t d)")
        xf, fT, yo, bias2 = (y_flat[:, n * UN * D:(n + 1) * UN * D].rearrange("p (s d) -> p s d", s=UN)
                             for n in range(4))
        w1 = xT_all[:, :, :].rearrange("p b n -> p (b n)")[:, 0:UN * WB].rearrange("p (s f) -> p s f", s=UN)

        SL = psum("SL", [P, 4, 512])
        PT = psum("PT", [P, 2, 512])
        O = psum("O", [P, 512])
        Q = psum("Q", [P, 512])
        slots = [SL[:, 2 * s:2 * s + 2, :].rearrange("p a n -> p (a n)") for s in range(2)]
        PTf = PT[:, :, :].rearrange("p a n -> p (a n)")
        slots.append(PTf)
        LG = (NT + 1) * P
        RK = LG + E

        ld_txt, ld_patch_W, ld_Wv, ld_attn, ld_small, ld_experts, ld_blank = (
            sem(n) for n in ("ld_txt", "ld_patch_W", "ld_Wv", "ld_attn", "ld_small", "ld_experts", "ld_blank"))
        ld_pixels = [sem(f"ld_pixels{half}") for half in range(2)]
        consts_ready = sem("consts_ready")
        settled_vec, settled_pool = sem("settled_vec"), sem("settled_pool")
        pool_step = sem("pool_step")
        vec_step = sem("vec_step")
        act_step = sem("act_step")
        patches_in_h = sem("patches_in_h")
        stat_ready = sem("stat_ready")
        rstd_ready = sem("rstd_ready")
        centred = sem("centred")
        squared = sem("squared")
        normed = sem("normed")
        pre_fill = sem("pre_fill")
        pre_evac = sem("pre_evac")
        beta_in_h = sem("beta_in_h")
        xs_ready = sem("xs_ready")
        filled = sem("filled")
        free = [sem(f"free{s}") for s in range(NSLOTS)]
        kh_done = sem("kh_done")
        q_psum = sem("q_psum")
        q_hi = sem("q_hi")
        q_lo = sem("q_lo")
        q_crossed_hi, q_crossed_lo = sem("q_crossed_hi"), sem("q_crossed_lo")
        z_done = sem("z_done")
        max_done = sem("max_done")
        exp_done = sem("exp_done")
        rden_done = sem("rden_done")
        p_normed = sem("p_normed")
        p_turned = sem("p_turned")
        pt_evac = sem("pt_evac")
        pv_done = sem("pv_done")
        y_done = sem("y_done")
        six_done, stat_done, rstd3_done, spread_done = (sem(n) for n in ("six_done", "stat_done", "rstd3_done", "spread_done"))
        scaled_done, h_done, x3_done, x3_turned, x3_evac = (
            sem(n) for n in ("scaled_done", "h_done", "x3_done", "x3_turned", "x3_evac"))
        stat_kept = sem("stat_kept")
        lg_done, lg_negated, lg_summed, largest_done, best_done, hot_ready, ranks_done = (sem(n) for n in (
            "lg_done", "lg_negated", "lg_summed", "largest_done", "best_done", "hot_ready", "ranks_done"))
        ranks_evac, placed, slot_found, counted, staged, pbest_done, skip_added, slot_ready = (sem(n) for n in (
            "ranks_evac", "placed", "slot_found", "counted", "staged", "pbest_done", "skip_added", "slot_ready"))
        experts_ready = sem("experts_ready")
        bases_ready = sem("bases_ready")
        rows_out = [sem(f"rows_out{t}") for t in range(NT)]
        SP_LOADS = [[0], [1], [2, 3], [4, 6], [8, 10, 12, 14, 16, 18, *range(20, SORTED)]]
        ACT_LOADS = [[5], [7, 11, 19]]
        POOL_LOADS = [[9, 13, 15, 17]]
        sp_rows_in = [sem(f"sp_rows_in{k}") for k in range(len(SP_LOADS))]
        act_rows_in = [sem(f"act_rows_in{k}") for k in range(len(ACT_LOADS))]
        pool_rows_in = [sem(f"pool_rows_in{k}") for k in range(len(POOL_LOADS))]
        loads = [*zip(SP_LOADS, sp_rows_in), *zip(ACT_LOADS, act_rows_in), *zip(POOL_LOADS, pool_rows_in)]
        assert sorted(i for group, _ in loads for i in group) == list(range(SORTED))
        b1_turned, b1_ready, gelu_loaded = sem("b1_turned"), sem("b1_ready"), sem("gelu_loaded")
        bias2_ready = sem("bias2_ready")
        w1_ready, xf_ready, f_turned, fT_ready, up_done, gelu_done, down_done, yb_done, yo_ready = (sem(n) for n in (
            "w1_ready", "xf_ready", "f_turned", "fT_ready", "up_done", "gelu_done", "down_done", "yb_done", "yo_ready"))
        out_done = [sem(f"out_done{s}") for s in range(UN)]

        out_rows = out.rearrange("b s d -> (b s) d")
        block = ctx.enter_context(nc.Block())

        def expert_tiles(eng):
            for i in range(2 * UN):
                yield i, i % UN, i // UN
            with eng.Fori(2, LOOPED) as u:
                at_u = eng.snap(u * UN)
                for s in range(UN):
                    yield at_u + s, s, u
            for i in range(LOOPED * UN, SORTED):
                yield i, i % UN, i // UN

        def load_tiles(eng, groups, loaded):
            eng.wait_ge(bases_ready, 1)
            for t in range(NT):
                eng.wait_ge(rows_out[t], 16 * (1 + len(range(t, TILES + 2, NT))))
            for group, done in zip(groups, loaded):
                for i in group:
                    base = eng.value_load(basei[0:1, i:i + 1], min_val=0, max_val=BLANK)
                    eng.dma_start(sorted_in[:, i, :], by_expert[bass.ds(base, P), :]).then_inc(done, 16)

        def later(i, n):
            return not isinstance(i, int) or i + n < SORTED

        @block.sync
        def _(sp):
            sp.dma_start(WtS, tok_W[:, :]).then_inc(ld_patch_W, 16)
            sp.dma_start(WvS[:, :], Wv).then_inc(ld_Wv, 16)
            for b in range(B):
                for c in range(C):
                    sp.dma_start(X[c * PX:(c + 1) * PX, b * GRID:(b + 1) * GRID, :],
                                 x[b, c].rearrange("(g i) w -> i g w", i=PX)).then_inc(ld_pixels[b * 2 // B], 16)
            sp.dma_start(WoS[:, :, :], Wo.rearrange("(h v) d -> v h d", v=D)).then_inc(ld_attn, 16)
            sp.dma_start(WkS[:, :], Wk).then_inc(ld_attn, 16)
            sp.dma_start(WqS[:, :], Wq).then_inc(ld_attn, 16)
            sp.dma_start(posS[0:NPATCH, :], pos[1:SEQ, :]).then_inc(ld_small, 16)
            sp.dma_start(posS[NPATCH:SEQ, :], pos[0:1, :]).then_inc(ld_small, 16)
            sp.dma_start(clsS[NPATCH:SEQ, :], cls_tok).then_inc(ld_small, 16)
            sp.dma_start(tbS[:, :], tok_b.unsqueeze(1)).then_inc(ld_small, 16)
            for t, v in ((boS, bo), (gammaS, gamma), (betaS, beta), (bsS, bs)):
                sp.dma_start(t[:, :], v.partition_broadcast(P)).then_inc(ld_small, 16)
            sp.dma_start(WsS[:, :], Ws).then_inc(ld_small, 16)
            sp.wait_ge(pre_fill, 6)
            w1_by_expert = W1S.rearrange("p (e f) -> p e f", e=E)
            sp.dma_start(w1_by_expert[:, :, 0:FF], W1.rearrange("e d f -> d e f")).then_inc(ld_experts, 16)
            sp.dma_start(W2S.rearrange("p (e n d) -> p e n d", e=E, n=NF),
                         W2.rearrange("e (n p) d -> p e n d", p=P)).then_inc(ld_experts, 16)
            sp.dma_start(w1_by_expert[:, :, FF + NF:WB], b2.partition_broadcast(P)).then_inc(ld_experts, 16)
            sp.dma_start(b1S, b1.rearrange("e (n p) -> (e n) p", p=P)).then_inc(ld_experts, 16)
            sp.wait_ge(consts_ready, 2)
            for e in range(E):
                sp.dma_start(by_expert[e * REGION:(e + 1) * REGION, :].rearrange("(t p) c -> p t c", p=P),
                             blank[:, :].unsqueeze(1).to_broadcast([P, REGION // P, ROW])).then_inc(ld_blank, 16)
            load_tiles(sp, SP_LOADS, sp_rows_in)

        @block.scalar
        def _(act):
            for b in range(B):
                act.dma_start(h_row[:, b * NT + 2:b * NT + 2 + NX, 0:D],
                              txt[b].rearrange("(t p) d -> p t d", p=P)).then_inc(ld_txt, 16)

            def squares(n, src, dst):
                act.wait_ge(centred, n)
                nc.scalar.activation(dst, src, ACT.Square).then_inc(squared, 1)

            sq_all = xT_all[:, :, :].rearrange("p b (t d) -> p b t d", t=NT)
            xn_v = xn_all[:, :, :].rearrange("p (b t) d -> p b t d", t=NT)
            def turned_patch_weights(g, fill):
                n = min(8, PX - 8 * g)
                act.wait_ge(pre_fill, fill)
                nc.scalar.activation(WtT[:, 8 * g:8 * g + n, :].rearrange("p j d -> p (j d)"),
                                     slots[g % 2][0:CI, 0:n * D], ACT.Copy).then_inc(pre_evac, 1)

            turned_patch_weights(0, 1)
            turned_patch_weights(1, 2)
            act.wait_ge(pre_fill, 3)
            nc.scalar.activation(WvT, slots[2], ACT.Copy).then_inc(pre_evac, 1)
            turned_patch_weights(2, 4)
            turned_patch_weights(3, 5)
            squares(1, xn_v[:, :, 0:NX, :], sq_all[:, :, 0:NX, :])
            act.wait_ge(pre_fill, 6)
            act.wait_ge(ld_small, 144)
            nc.scalar.activation(tokT[:, :], Q[:, 0:B * NPATCH], ACT.Identity, bias=tbS[:, 0:1]).then_inc(pre_evac, 1)
            act.wait_ge(pre_fill, 8)
            nc.scalar.activation(VO[:, :], slots[2], ACT.Copy).then_inc(pre_evac, 1)
            for b in range(B):
                act.wait_ge(pre_fill, 9 + b)
                nc.scalar.activation(xT_all[:, b - 1, 0:NX * P] if b > 0 else xs[:, 0:NX * P],
                                     slots[b % 2][:, 0:NX * P], ACT.Copy).then_inc(pre_evac, 1)
                if b == 1:
                    squares(2, xn_v[:, :, NX, :], sq_all[:, :, NX, :])
            act.wait_ge(pre_fill, 9 + B)
            nc.scalar.activation(xs[:, NX * P:NT * P], O[:, 0:P], ACT.Copy).then_inc(xs_ready, 1)
            nc.scalar.activation(xT_all[:, 0:B - 1, NX * P:NT * P], O[:, P:B * P].rearrange("p (b n) -> p b n", n=P),
                                 ACT.Copy).then_inc(pre_evac, 1)

            def sum_logits(row):
                act.wait_ge(lg_negated, row + 1)
                nc.scalar.activation(lg_exp[:, :], neg_lg[:, :], ACT.Exp, bias=neg_max[:, 0:1], scale=-1.0,
                                     accum_out=lg_den[:, 0:1]).then_inc(lg_summed, 1)

            with act.Fori(0, B) as b:
                at_fill = act.snap(b * FILLS)
                at_step = act.snap(b * STEPS)
                at_tile = act.snap(b * NT)
                at_slot = [act.snap(b * n) for n in PER_SLOT]
                for h in range(H):
                    n, slot, _ = FILL["keys", h // 2]
                    half = slice(h % 2 * K, h % 2 * K + K)
                    act.wait_ge(filled, at_fill + (n + 1))
                    nc.scalar.activation(KHL[0:K, h, :], slots[slot][half, AT:AT + SP], ACT.Copy).then_inc(kh_done, 1)

                def queries(t, par):
                    act.wait_ge(q_psum, at_tile + (t + 2))
                    nc.scalar.activation(QS[0:K, t % 2, par::2, :],
                                         Q[K * par:K * par + K, :].rearrange("p (i m) -> p i m", m=P),
                                         ACT.Copy).then_inc(q_hi, 1)
                    act.wait_ge(q_hi, (at_tile + t) * 2 + (par + 1))
                    nc.scalar.activation(QX[K:2 * K, t % 2, par::2, :], QS[0:K, t % 2, par::2, :].bitcast(F32),
                                         ACT.Copy).then_inc(q_crossed_hi, 1)

                queries(0, 0)
                queries(0, 1)

                def copy_scores(g):
                    n, slot, _ = FILL["scores", g]
                    act.wait_ge(filled, at_fill + (n + 1))
                    if g >= 2:
                        act.wait_ge(exp_done, at_step + (g - 1))
                    nc.scalar.activation(score[:, g % 2, :], slots[slot][:, AT:AT + S], ACT.Copy).then_inc(free[slot], 1)

                def exponentials(g):
                    act.wait_ge(max_done, at_step + (g + 1))
                    if g >= 2:
                        act.wait_ge(p_normed, at_step + (g - 1))
                        act.wait_ge(rden_done, at_step + (g - 1))
                    nc.scalar.activation(prob[:, g % 2, :], score[:, g % 2, :], ACT.Exp, bias=rmax[:, g % 2:g % 2 + 1],
                                         scale=-1.0, accum_out=den[:, g % 2:g % 2 + 1]).then_inc(exp_done, 1)

                def evacuate(g):
                    act.wait_ge(p_turned, at_step + (g + 1))
                    if g >= 2:
                        act.wait_ge(pv_done, at_step + g)
                    nc.scalar.activation(pT[:, g % 2, :], PTf[:, 0:NT * P], ACT.Copy).then_inc(pt_evac, 1)

                def values(t):
                    n, slot, _ = FILL["values", t]
                    act.wait_ge(filled, at_fill + (n + 1))
                    nc.scalar.activation(Vt[:, t, :], slots[slot], ACT.Copy).then_inc(free[slot], 1)

                values(0)
                copy_scores(0)
                copy_scores(1)
                exponentials(0)
                values(2)
                copy_scores(2)
                exponentials(1)
                values(4)
                for g in range(STEPS):
                    if g >= 2:
                        exponentials(g)
                    if 1 <= g < STEPS - 2:
                        copy_scores(g + 2)
                    if g % 2 == 1:
                        evacuate(g - 1)
                    if g % H in QSTEPS_ACT and g // H + 1 < NT:
                        queries(g // H + 1, QSTEPS_ACT.index(g % H))
                    if g % H == 3:
                        sum_logits(at_tile + g // H)
                    if g == STEPS - 4:
                        act.wait_ge(pre_evac, 8 + B)
                        act.wait_ge(q_lo, (at_tile + NT) * 2 + 1)
                        nc.scalar.activation(xs[:, :], xT_all[:, bass.ds(b, 1), :].rearrange("p a n -> p (a n)"),
                                             ACT.Copy).then_inc(xs_ready, 1)

            sum_logits(TILES)
            act.wait_ge(x3_turned, TILES + 2)
            nc.scalar.activation(x3T[:, :], PTf[:, NT * P:(NT + 1) * P], ACT.Copy).then_inc(x3_evac, 1)
            act.wait_ge(pbest_done, TILES + 1)
            sum_logits(TILES + 1)
            act.wait_ge(lg_summed, TILES + 2)
            nc.scalar.activation(lg_exp[:, :], neg_lg[:, :], ACT.Gelu).then_inc(gelu_loaded, 1)

            def evacuate_turned(i, s):
                act.wait_ge(f_turned, i + 1)
                nc.scalar.activation(fT[:, s, :], Q[:, 0:P], ACT.Copy).then_inc(fT_ready, 1)

            def gelu(i, s):
                act.wait_ge(up_done, i + 1)
                for c in range(NF):
                    last = nc.scalar.activation(hidT[:, s, c * P:(c + 1) * P], SL[:, s, c * P:(c + 1) * P], ACT.Gelu,
                                                bias=w1[:, s, FF + c:FF + c + 1])
                last.then_inc(gelu_done, 1)

            load_tiles(act, ACT_LOADS, act_rows_in)
            evacuate_turned(0, 0)
            evacuate_turned(1, 1)
            gelu(0, 0)
            evacuate_turned(2, 2)
            for i, s, _ in expert_tiles(act):
                if later(i, 1):
                    gelu(i + 1, (s + 1) % UN)
                if later(i, 3):
                    evacuate_turned(i + 3, (s + 3) % UN)

        @block.gpsimd
        def _(pool):
            pool.sem_inc(q_psum)
            n_step = [0]

            def settle_pool():
                pool.sem_inc(settled_pool)


            def step(ins):
                n_step[0] += 1
                ins.then_inc(pool_step, 1)
                pool.wait_ge(pool_step, n_step[0])

            step(nc.gpsimd.memset(ident[:, :], 0.0))
            step(nc.gpsimd.affine_select(out=ident[:, :], in_=ident[:, :], compare_op=ALU.not_equal, fill=1.0, base=0,
                                         pattern=[[-1, P]], channel_multiplier=1))
            step(nc.gpsimd.memset(minus_one[:, :], -1.0))
            nc.gpsimd.memset(half[:, :], -0.5).then_inc(consts_ready, 1)
            step(nc.gpsimd.memset(blank[:, :], 0.0))
            nc.gpsimd.memset(blank[:, TOKEN:TOKEN + 1].bitcast(I32), SKIP).then_inc(consts_ready, 1)
            step(nc.gpsimd.memset(eps2[:, 0:1], 1e-6))
            step(nc.gpsimd.memset(eps2[:, 1:2], 1e-5))
            step(nc.gpsimd.memset(ones, 1.0))
            step(nc.gpsimd.affine_select(out=before, in_=ones, compare_op=ALU.is_gt, fill=0.0, base=0,
                                         pattern=[[1, P]], channel_multiplier=-1))
            step(nc.gpsimd.iota(rampi[:, :], pattern=[[1, 32]], base=0, channel_multiplier=0))
            tid = tokid[:, :].rearrange("p (b t) -> p b t", t=NT)
            step(nc.gpsimd.iota(tid[:, :, 0:NX], pattern=[[S, B], [P, NX]], base=SEQ, channel_multiplier=1))
            step(nc.gpsimd.iota(tid[:, :, NX], pattern=[[S, B]], base=1, channel_multiplier=1))
            step(nc.gpsimd.iota(tid[NPATCH:SEQ, :, NX], pattern=[[S, B]], base=0, channel_multiplier=0))
            step(nc.gpsimd.memset(valid[:, :], 1.0))
            step(nc.gpsimd.memset(valid[:, 0:2], 0.0))
            nc.gpsimd.affine_select(out=valid[:, 2 + NX::NT], in_=valid[:, 2 + NX::NT], compare_op=ALU.is_gt, fill=0.0,
                                    base=SEQ, pattern=[[0, B]], channel_multiplier=-1).then_inc(consts_ready, 1)
            for t in range(NT):
                pool.dma_start(by_expert[BLANK + t * P:BLANK + (t + 1) * P, :], blank[:, :]).then_inc(rows_out[t], 16)
            rs = rstd[:, :].rearrange("p (b t) -> p b t", t=NT)
            vs = var[:, :].rearrange("p (b t) -> p b t", t=NT)
            hs = half[:, :].rearrange("p (b t) -> p b t", t=NT)
            for n, part in enumerate((slice(0, NX), slice(NX, NT))):
                pool.wait_ge(stat_ready, n + 1)
                nc.gpsimd.tensor_tensor(rs[:, :, part], vs[:, :, part], hs[:, :, part], ALU.pow).then_inc(rstd_ready, 1)
            pool.wait_ge(normed, 2)
            pool.wait_ge(ld_small, 144)
            nc.gpsimd.tensor_tensor(h_all, h_all, betaS[:, :].unsqueeze(1).to_broadcast([P, TILES, D]), ALU.add)\
                .then_inc(beta_in_h, 1)

            def power(n, row):
                variance = (stat, stat3)[n][:, 1:2]
                pool.wait_ge(stat_done, row * 2 + (n + 1))
                nc.gpsimd.tensor_tensor(spread[:, n:n + 1], variance, eps2[:, n:n + 1], ALU.add)\
                    .then_inc(spread_done, 1)
                pool.wait_ge(spread_done, row * 2 + (n + 1))
                nc.gpsimd.tensor_tensor(variance, spread[:, n:n + 1], half[:, 0:1], ALU.pow).then_inc(rstd3_done, 1)
                if n == 1:
                    pool.wait_ge(rstd3_done, row * 2 + 2)
                    settle_pool()
                    nc.gpsimd.tensor_copy(h_row[:, bass.ds(row + 1, 1), MEAN:MEAN + 2].rearrange("p a c -> p (a c)"),
                                          stat3[:, :]).then_inc(stat_kept, 1)

            def stage_rows(row, t):
                before_it = row // NT if isinstance(row, int) else None
                pool.wait_ge(rows_out[t], 16 * (before_it + 1) if before_it is not None else at_batch + 16)
                settle_pool()
                nc.gpsimd.tensor_copy(row_stage[:, t, :], h_row[:, bass.ds(row, 1), :].rearrange("p a c -> p (a c)"))\
                    .then_inc(staged, 1)
                pool.wait_ge(staged, row + 1)
                pool.wait_ge(lg_summed, row + 1)
                nc.gpsimd.tensor_tensor(row_stage[:, t, PBEST:PBEST + 1], lg_den[:, :], minus_one[:, :], ALU.pow)\
                    .then_inc(pbest_done, 1)

            def scatter_rows(row, t):
                pool.wait_ge(slot_found, row + 1)
                settle_pool()
                nc.gpsimd.tensor_tensor(slot_or_skip[:, :], slotf[:, :], skip[:, bass.ds(row, 1)], ALU.add)\
                    .then_inc(skip_added, 1)
                pool.wait_ge(skip_added, row + 1)
                settle_pool()
                nc.gpsimd.tensor_copy(slotu[:, t:t + 1], slot_or_skip[:, :]).then_inc(slot_ready, 1)
                pool.wait_ge(ld_blank, 16 * E)
                pool.wait_ge(pbest_done, row + 1)
                pool.wait_ge(slot_ready, row + 1)
                settle_pool()
                nc.gpsimd.indirect_dma_start(
                    out=by_expert[:, :], out_offset=bass.IndirectOffsetOnAxis(ap=slotu[:, t:t + 1], axis=0),
                    in_=row_stage[:, t, :], in_offset=None, bounds_check=BLANK - 1, oob_is_err=False)\
                    .then_inc(rows_out[t], 16)

            with pool.Fori(0, B) as b:
                at_batch = pool.snap(b * 16)
                at_step = pool.snap(b * STEPS)
                at_tile = pool.snap(b * NT)

                for g in range(STEPS):
                    pool.wait_ge(rden_done, at_step + (g + 1))
                    if g >= 2:
                        pool.wait_ge(p_turned, at_step + (g - 1))
                    settle_pool()
                    nc.gpsimd.tensor_scalar(pn[:, g % 2, 0:S], prob[:, g % 2, :], rden[:, g % 2:g % 2 + 1], 1.0,
                                            ALU.mult, ALU.mult).then_inc(p_normed, 1)
                    row = at_tile + g // H
                    if g % H == POW2:
                        power(0, row)
                    if g % H == POW3:
                        power(1, row)
                    if g % H == 5:
                        stage_rows(row, g // H)
                    if g % H == 7:
                        scatter_rows(row, g // H)
            power(0, TILES)
            power(1, TILES)
            for n in range(2):
                stage_rows(TILES + n, n)
                scatter_rows(TILES + n, n)
            load_tiles(pool, POOL_LOADS, pool_rows_in)
            for i, s, _ in expert_tiles(pool):

                pool.wait_ge(yo_ready, i + 1)
                settle_pool()
                nc.gpsimd.indirect_dma_start(
                    out=out_rows, out_offset=bass.IndirectOffsetOnAxis(ap=idx[:, s:s + 1], axis=0),
                    in_=yo[:, s, :], in_offset=None, bounds_check=TOKENS - 1, oob_is_err=False)\
                    .then_inc(out_done[s], 16)
            for s in range(UN):
                pool.wait_ge(out_done[s], 16 * len(range(s, SORTED, UN)))

        @block.vector
        def _(dve):
            dve.sem_inc(pv_done)
            dve.sem_inc(x3_turned)
            dve.sem_inc(stat_kept)
            dve.sem_inc(counted)
            n_step = [0]

            def settle_vec():
                dve.sem_inc(settled_vec)


            def step(ins):
                n_step[0] += 1
                ins.then_inc(vec_step, 1)
                dve.wait_ge(vec_step, n_step[0])

            h_v = h_all.rearrange("p (b t) d -> p b t d", t=NT)
            xn_v = xn_all[:, :, :].rearrange("p (b t) d -> p b t d", t=NT)
            sq_v = xT_all[:, :, :].rearrange("p b (t d) -> p b t d", t=NT)
            mean_v = mean[:, :].rearrange("p (b t) -> p b t", t=NT)
            var_v = var[:, :].rearrange("p (b t) -> p b t", t=NT)
            rstd_v = rstd[:, :].rearrange("p (b t) -> p b t", t=NT)

            def wide(a, like):
                return a.unsqueeze(len(a.shape)).to_broadcast(list(like.shape))

            def normalise(n, src, cen, sq, m, v, r, eps, last=None):
                step(nc.vector.tensor_reduce(m, src, AX.X, ALU.add))
                step(nc.vector.tensor_scalar(m, m, 1.0 / D, None, ALU.mult))
                nc.vector.tensor_tensor(cen, src, wide(m, src), ALU.subtract).then_inc(centred, 1)
                dve.wait_ge(squared, n)
                step(nc.vector.tensor_reduce(v, sq, AX.X, ALU.add))
                nc.vector.tensor_scalar(v, v, 1.0 / D, eps, ALU.mult, ALU.add).then_inc(stat_ready, 1)
                dve.wait_ge(rstd_ready, n)
                nc.vector.tensor_tensor(cen, cen, wide(r, src), ALU.mult).then_inc(normed, 1)
                dve.wait_ge(normed, n)

            step(nc.vector.memset(h_v[NPATCH:P, :, NX, :], 0.0))
            step(nc.vector.memset(h_row[:, 0:2, :], 0.0))
            step(nc.vector.memset(h_row[:, 2:, D:ROW], 0.0))
            step(nc.vector.memset(y_row[:, 0, :], 0.0))
            step(nc.vector.memset(x3T[:, :], 0.0))
            step(nc.vector.memset(pn[:, :, S:NT * P], 0.0))
            dve.wait_ge(ld_txt, 16 * B)
            normalise(1, h_v[:, :, 0:NX, :], xn_v[:, :, 0:NX, :], sq_v[:, :, 0:NX, :],
                      mean_v[:, :, 0:NX], var_v[:, :, 0:NX], rstd_v[:, :, 0:NX], 1e-5)
            dve.wait_ge(ld_small, 144)

            step(nc.vector.tensor_tensor(h_v[NPATCH:SEQ, :, NX, :],
                                         clsS[NPATCH:SEQ, :].unsqueeze(1).to_broadcast([1, B, D]),
                                         posS[NPATCH:SEQ, :].unsqueeze(1).to_broadcast([1, B, D]), ALU.mult))
            dve.wait_ge(pre_fill, 7)
            step(nc.vector.tensor_tensor(h_v[0:NPATCH, :, NX, :],
                                         O[0:NPATCH, :].rearrange("p (b d) -> p b d", b=B),
                                         posS[0:NPATCH, :].unsqueeze(1).to_broadcast([NPATCH, B, D]), ALU.mult))
            normalise(2, h_v[:, :, NX, :], xn_v[:, :, NX, :], sq_v[:, :, NX, :],
                      mean_v[:, :, NX], var_v[:, :, NX], rstd_v[:, :, NX], 1e-5)

            dve.wait_ge(consts_ready, 3)
            step(nc.vector.tensor_copy(before_r[:, :], before))
            step(nc.vector.tensor_copy(ones_r[:, :], ones))
            step(nc.vector.tensor_copy(h_row[:, 2:, TOKEN].bitcast(I32), tokid[:, :]))
            step(nc.vector.tensor_copy(ramp[:, :], rampi[:, :]))
            step(nc.vector.tensor_scalar(rampP[:, :], ramp[:, :], float(P), None, ALU.mult))
            step(nc.vector.tensor_scalar(beyond[:, :], rampP[:, :], -1.0, float(BLANK), ALU.mult, ALU.add))
            step(nc.vector.tensor_scalar(order[:, :], ramp[:, 0:E], -1.0, float(E), ALU.mult, ALU.add))
            step(nc.vector.tensor_scalar(region[:, :], ramp[:, 0:E], float(REGION), None, ALU.mult))
            step(nc.vector.tensor_scalar(running[:, :], ramp[:, 0:E], float(REGION), None, ALU.mult))
            step(nc.vector.memset(one8[:, :], 1.0))
            step(nc.vector.tensor_scalar(skip[:, :], valid[:, :], -float(SKIP), float(SKIP), ALU.mult, ALU.add))

            step(nc.vector.tensor_tensor(y_all, xn_all[:, :, :], boS[:, :].unsqueeze(1).to_broadcast([P, TILES, D]),
                                         ALU.add))
            dve.wait_ge(pre_evac, 8 + B)
            step(nc.vector.memset(O[:, 0:D], 0.0))

            def tile_row(row, c, n):
                return h_row[:, bass.ds(row + 1, 1), c:c + n].rearrange("p a d -> p (a d)")

            def attention_residual(row, steps):
                dve.wait_ge(pv_done, steps + 1)
                y = y_row[:, bass.ds(row, 1), :].rearrange("p a d -> p (a d)")
                nc.vector.tensor_tensor(y, O[:, 0:D], y, ALU.add).then_inc(y_done, 1)

            def sums(row, n):
                if n == 0:
                    dve.wait_ge(y_done, row + 1)
                    src = y_row[:, bass.ds(row, 1), :].rearrange("p a d -> p (a d)")
                else:
                    dve.wait_ge(h_done, row + 1)
                    dve.wait_ge(stat_kept, row + 1)
                    src = tile_row(row, 0, D)
                settle_vec()
                nc.vector.bn_stats(six[:, :], src).then_inc(six_done, 1)

            def mean_and_variance(row, n):
                dve.wait_ge(six_done, row * 2 + (n + 1))
                settle_vec()
                nc.vector.bn_aggr((stat, stat3)[n][:, :], six[:, :]).then_inc(stat_done, 1)

            def scale(row):
                dve.wait_ge(rstd3_done, row * 2 + 1)
                y = y_row[:, bass.ds(row, 1), :].rearrange("p a d -> p (a d)")
                nc.vector.scalar_tensor_tensor(out=scaled[:, :], in0=y, scalar=stat[:, 0:1], in1=gammaS[:, :],
                                               op0=ALU.subtract, op1=ALU.mult).then_inc(scaled_done, 1)

            def add_residual(row):
                dve.wait_ge(beta_in_h, 1)
                dve.wait_ge(scaled_done, row + 1)
                h = tile_row(row, 0, D)
                nc.vector.scalar_tensor_tensor(out=h, in0=scaled[:, :], scalar=stat[:, 1:2], in1=h,
                                               op0=ALU.mult, op1=ALU.add).then_inc(h_done, 1)

            def third_normalisation(row):
                dve.wait_ge(rstd3_done, row * 2 + 2)
                dve.wait_ge(x3_turned, row + 1)
                nc.vector.tensor_scalar(x3[:, :], tile_row(row, 0, D), stat3[:, 0:1], stat3[:, 1:2],
                                        ALU.subtract, ALU.mult).then_inc(x3_done, 1)

            def negate_logits(row):
                dve.wait_ge(lg_done, row + 1)
                settle_vec()
                nc.vector.tensor_tensor_reduce(neg_lg[:, :], PTf[:, LG:LG + E], bsS[:, :], -1.0, 3e38,
                                               ALU.add, ALU.min, neg_max[:, 0:1]).then_inc(lg_negated, 1)

            def mark_largest(row):
                dve.wait_ge(lg_negated, row + 1)
                nc.vector.tensor_scalar(largest[:, :], neg_lg[:, :], neg_max[:, 0:1], 1.0, ALU.is_equal, ALU.mult)\
                    .then_inc(largest_done, 1)

            def highest_order(row):
                dve.wait_ge(largest_done, row + 1)
                settle_vec()
                nc.vector.tensor_tensor_reduce(largest[:, :], largest[:, :], order[:, :], 1.0, 0.0,
                                               ALU.mult, ALU.max, best[:, 0:1]).then_inc(best_done, 1)

            def choose_expert(row):
                dve.wait_ge(best_done, row + 1)
                nc.vector.tensor_scalar(hot[:, :], order[:, :], best[:, 0:1], valid[:, bass.ds(row, 1)],
                                        ALU.is_equal, ALU.mult).then_inc(hot_ready, 1)

            def evacuate_ranks(row):
                dve.wait_ge(ranks_done, row + 1)
                nc.vector.tensor_copy(ranks[:, :], PTf[:, RK:RK + 2 * E]).then_inc(ranks_evac, 1)

            def places_by_expert(row):
                dve.wait_ge(ranks_evac, row + 1)
                nc.vector.tensor_tensor(place[:, :], ranks[:, 0:E], running[:, :], ALU.add).then_inc(placed, 1)

            def find_places(row):
                dve.wait_ge(placed, row + 1)
                settle_vec()
                nc.vector.tensor_tensor_reduce(place[:, :], place[:, :], hot[:, :].bitcast(F32), 1.0, 0.0,
                                               ALU.mult, ALU.max, slotf[:, 0:1]).then_inc(slot_found, 1)
                nc.vector.tensor_tensor(running[:, :], ranks[:, E:2 * E], running[:, :], ALU.add)\
                    .then_inc(counted, 1)

            with dve.Fori(0, B) as b:
                at_fill = dve.snap(b * FILLS)
                at_step = dve.snap(b * STEPS)
                at_tile = dve.snap(b * NT)
                at_head = dve.snap(b * H)
                at_slot = [dve.snap(b * n) for n in PER_SLOT]
                for h in range(H):
                    _, slot, _ = FILL["keys", h // 2]
                    half = slice(h % 2 * K, h % 2 * K + K)
                    dve.wait_ge(kh_done, at_head + (h + 1))
                    last = nc.vector.tensor_tensor(KHL[K:2 * K, h, :], slots[slot][half, AT:AT + SP],
                                                   KHL[0:K, h, :].bitcast(F32), ALU.subtract)
                    if h % 2 == 1:
                        last.then_inc(free[slot], 1)

                def queries(t, par):
                    dve.wait_ge(q_hi, (at_tile + t) * 2 + (par + 1))
                    nc.vector.tensor_tensor(QS[K:2 * K, t % 2, par::2, :],
                                            Q[K * par:K * par + K, :].rearrange("p (i m) -> p i m", m=P),
                                            QS[0:K, t % 2, par::2, :].bitcast(F32), ALU.subtract).then_inc(q_lo, 1)

                def cross_queries(t, par):
                    dve.wait_ge(q_lo, (at_tile + t) * 2 + (par + 2))
                    nc.vector.tensor_copy(QX[0:K, t % 2, par::2, :], QS[K:2 * K, t % 2, par::2, :])\
                        .then_inc(q_crossed_lo, 1)

                queries(0, 0)
                queries(0, 1)
                cross_queries(0, 0)
                cross_queries(0, 1)

                def reciprocals(g):
                    dve.wait_ge(exp_done, at_step + (g + 1))
                    if g >= 2:
                        dve.wait_ge(p_normed, at_step + (g - 1))
                    nc.vector.reciprocal(rden[:, g % 2:g % 2 + 1], den[:, g % 2:g % 2 + 1]).then_inc(rden_done, 1)

                def mask_and_max(g, between=()):
                    _, slot, k = FILL["scores", g]
                    dve.wait_ge(free[slot], at_slot[slot] + (k + 2))
                    if g >= 1:
                        dve.wait_ge(max_done, at_step + g)
                    nc.vector.tensor_scalar(zero_mark[:, :], score[:, g % 2, :], 0.0, -1e9 * K ** 0.5,
                                            ALU.is_equal, ALU.mult).then_inc(z_done, 1)
                    for operation in between:
                        operation()
                    dve.wait_ge(z_done, at_step + (g + 1))
                    settle_vec()
                    nc.vector.tensor_tensor_reduce(score[:, g % 2, :], score[:, g % 2, :], zero_mark[:, :],
                                                   -(K ** -0.5), 3e38, ALU.add, ALU.min,
                                                   rmax[:, g % 2:g % 2 + 1]).then_inc(max_done, 1)

                def evacuate(g):
                    dve.wait_ge(p_turned, at_step + (g + 1))
                    if g >= 2:
                        dve.wait_ge(pv_done, at_step + g)
                    if g % H == 7:
                        nc.vector.tensor_copy(x3T[:, :], PTf[:, NT * P:(NT + 1) * P]).then_inc(x3_evac, 1)
                    if g % H == 1:
                        negate_logits(at_tile + g // H)
                    if g % H == 5:
                        evacuate_ranks(at_tile + g // H)
                    nc.vector.tensor_copy(pT[:, g % 2, :], PTf[:, 0:NT * P]).then_inc(pt_evac, 1)

                def values(t):
                    n, slot, _ = FILL["values", t]
                    dve.wait_ge(filled, at_fill + (n + 1))
                    nc.vector.tensor_copy(Vt[:, t, :], slots[slot]).then_inc(free[slot], 1)

                values(1)
                mask_and_max(0)
                mask_and_max(1)
                reciprocals(0)
                values(3)
                reciprocals(1)
                for g in range(STEPS):
                    row = at_tile + g // H
                    between = {
                        3: [lambda: mark_largest(row), lambda: sums(row, 0)],
                        4: [lambda: highest_order(row), lambda: mean_and_variance(row, 0)],
                        5: [lambda: choose_expert(row), lambda: scale(row)],
                        6: [lambda: sums(row, 1)],
                        7: [lambda: places_by_expert(row)],
                    }.get(g % H, [])
                    if g % H - 1 in QSTEPS_VEC and g // H + 1 < NT:
                        between = between + [lambda: cross_queries(g // H + 1, QSTEPS_VEC.index(g % H - 1))]
                    if 1 <= g < STEPS - 1:
                        mask_and_max(g + 1, between)
                    else:
                        for operation in between:
                            operation()
                    if g >= 2:
                        reciprocals(g)
                    if g % H == 2:
                        attention_residual(row, at_step + g // H * H)
                    if g >= 1 and (g - 1) % 2 == 1:
                        evacuate(g - 1)
                    if g % H in QSTEPS_VEC and g // H + 1 < NT:
                        queries(g // H + 1, QSTEPS_VEC.index(g % H))
                    if g % H == 5:
                        add_residual(row)
                    if g % H == 6:
                        mean_and_variance(row, 1)
                    if g % H == 7:
                        third_normalisation(row)
                        find_places(row)
                evacuate(STEPS - 1)

            attention_residual(TILES, B * STEPS)
            sums(TILES, 0)
            dve.wait_ge(b1_turned, 1)
            nc.vector.tensor_copy(W1S.rearrange("p (e f) -> p e f", e=E)[:, :, FF:FF + NF],
                                  Q[:, 0:E * NF].rearrange("p (e n) -> p e n", e=E)).then_inc(b1_ready, 1)
            negate_logits(TILES)
            mean_and_variance(TILES, 0)
            mark_largest(TILES)
            highest_order(TILES)
            choose_expert(TILES)
            scale(TILES)
            add_residual(TILES)
            sums(TILES, 1)
            mean_and_variance(TILES, 1)
            evacuate_ranks(TILES)
            places_by_expert(TILES)
            find_places(TILES)
            third_normalisation(TILES)
            negate_logits(TILES + 1)
            mark_largest(TILES + 1)
            highest_order(TILES + 1)
            choose_expert(TILES + 1)
            evacuate_ranks(TILES + 1)
            places_by_expert(TILES + 1)
            dve.wait_ge(skip_added, TILES + 1)
            find_places(TILES + 1)
            dve.wait_ge(counted, TILES + 3)

            step(nc.vector.tensor_tensor(tstart[:, :], running[:, :], region[:, :], ALU.subtract))
            step(nc.vector.tensor_tensor(full[:, :, :], wide(tstart[:, :], full[:, :, :]),
                                         rampP[:, 0:TILES].unsqueeze(1).to_broadcast([P, E, TILES]), ALU.is_gt))
            step(nc.vector.tensor_reduce(ntile[:, :], full[:, :, :], AX.X, ALU.add))
            step(nc.vector.tensor_tensor_scan(tend[:, :], one8[:, :], ntile[:, :], 0.0, ALU.mult, ALU.add))
            every = [P, SORTED, E]
            number = wide(ramp[:, 0:SORTED], ended)
            step(nc.vector.tensor_tensor(ended, number, tend[:, :].unsqueeze(1).to_broadcast(every), ALU.is_ge))
            step(nc.vector.tensor_tensor(tstart[:, :], tend[:, :], ntile[:, :], ALU.subtract))
            step(nc.vector.tensor_tensor(within, number, tstart[:, :].unsqueeze(1).to_broadcast(every), ALU.is_ge))
            step(nc.vector.tensor_tensor(within, within, ended, ALU.subtract))
            step(nc.vector.scalar_tensor_tensor(out=tstart[:, :], in0=tstart[:, :], scalar=-float(P), in1=region[:, :],
                                                op0=ALU.mult, op1=ALU.add))
            step(nc.vector.tensor_tensor(within, within, tstart[:, :].unsqueeze(1).to_broadcast(every), ALU.mult))
            step(nc.vector.tensor_reduce(basef[:, :], within, AX.X, ALU.add))
            step(nc.vector.tensor_tensor(basef[:, :], basef[:, :], rampP[:, 0:SORTED], ALU.add))
            step(nc.vector.tensor_tensor(exf[:, :], ended[:, :, E - 1], beyond[:, 0:SORTED], ALU.mult))
            step(nc.vector.tensor_tensor(basef[:, :], basef[:, :], exf[:, :], ALU.add))
            nc.vector.tensor_copy(basei[:, :], basef[:, :]).then_inc(bases_ready, 1)
            step(nc.vector.tensor_reduce(exf[:, :], ended, AX.X, ALU.add))
            step(nc.vector.tensor_scalar(exf[:, :], exf[:, :], float(E - 1), None, ALU.min))
            nc.vector.tensor_copy(exi[:, :], exf[:, :]).then_inc(experts_ready, 1)

            dve.wait_ge(experts_ready, 1)
            dve.wait_ge(ld_experts, 16 * 4)

            def row_of(i, c, n):
                return sorted_in[:, bass.ds(i, 1), c:c + n].rearrange("p a c -> p (a c)")

            def expert(i):
                return dve.value_load(exi[0:1, bass.ds(i, 1)], min_val=0, max_val=E - 1)

            def normalise_rows(i, s):
                nc.vector.tensor_scalar(xf[:, s, :], row_of(i, 0, D), row_of(i, MEAN, 1), row_of(i, RSTD, 1),
                                        ALU.subtract, ALU.mult).then_inc(xf_ready, 1)

            def down(i, s, turns):
                dve.wait_ge(down_done, i + 1)
                if not isinstance(turns, int) or turns > 0:
                    dve.wait_ge(out_done[s], turns * 16)
                nc.vector.tensor_tensor(yo[:, s, :], O[:, 0:D], bias2[:, s, :], ALU.add).then_inc(yb_done, 1)
                nc.vector.tensor_copy(idx[:, s:s + 1], row_of(i, TOKEN, 1).bitcast(U32)).then_inc(yb_done, 1)
                dve.wait_ge(yb_done, i * 2 + 2)
                nc.vector.scalar_tensor_tensor(out=yo[:, s, :], in0=yo[:, s, :], scalar=row_of(i, PBEST, 1),
                                               in1=row_of(i, 0, D), op0=ALU.mult, op1=ALU.add).then_inc(yo_ready, 1)

            def keep_bias(i, s):
                dve.wait_ge(w1_ready, i + 1)
                nc.vector.tensor_copy(bias2[:, s, :], w1[:, s, FF + NF:WB]).then_inc(bias2_ready, 1)

            def expert_weights(i, s):
                nc.vector.tensor_copy(w1[:, s, :], W1S[:, bass.ds(expert(i) * WB, WB)]).then_inc(w1_ready, 1)

            dve.wait_ge(b1_ready, 1)
            def wait_loads(first, end):
                for group, loaded in loads:
                    if first <= group[0] < end:
                        dve.wait_ge(loaded, 16 * len(group))

            for i in range(UN):
                expert_weights(i, i)
                wait_loads(i, i + 1)
                normalise_rows(i, i)
            keep_bias(0, 0)
            keep_bias(1, 1)
            dve.wait_ge(f_turned, 1)
            normalise_rows(3, 0)
            for i, s, turns in expert_tiles(dve):
                if isinstance(i, int) and i < 2 * UN:
                    wait_loads(i + AHEAD, i + AHEAD + 1 if i + 1 < 2 * UN else SORTED)
                if later(i, AHEAD):
                    dve.wait_ge(f_turned, i + 2)
                    normalise_rows(i + AHEAD, (s + AHEAD) % UN)
                if later(i, 2):
                    keep_bias(i + 2, (s + 2) % UN)
                if later(i, UN):
                    dve.wait_ge(gelu_done, i + 1)
                    dve.wait_ge(bias2_ready, i + 1)
                    expert_weights(i + UN, s)
                down(i, s, turns)

        @block.tensor
        def _(pe):
            for primed in (*free, q_lo, x3_evac):
                pe.sem_inc(primed)
            pe.wait_ge(consts_ready, 1)
            def turn_patch_weights(g):
                for j in range(min(8, PX - 8 * g)):
                    last = nc.tensor.transpose(slots[g % 2][0:CI, j * D:(j + 1) * D], WtS[:, 8 * g + j::PX], ident[:, :])
                last.then_inc(pre_fill, 1)

            pe.wait_ge(ld_patch_W, 16)
            turn_patch_weights(0)
            turn_patch_weights(1)
            pe.wait_ge(ld_Wv, 16)
            for h in range(H):
                last = nc.tensor.transpose(slots[2][:, h * D:(h + 1) * D], WvS[:, h * D:(h + 1) * D], ident[:, :])
            last.then_inc(pre_fill, 1)
            pe.wait_ge(pre_evac, 1)
            turn_patch_weights(2)
            pe.wait_ge(pre_evac, 2)
            turn_patch_weights(3)
            pe.wait_ge(pre_evac, 5)
            Xv = X.rearrange("p g (w j) -> p g w j", j=PX)
            for part in range(2):
                pe.wait_ge(ld_pixels[part], 16 * (B // 2) * C)
                rows = slice(part * (B // 2) * GRID, (part + 1) * (B // 2) * GRID)
                for j in range(PX):
                    last = nc.tensor.matmul(Q[:, 0:B * NPATCH].rearrange("p (g w) -> p g w", w=GRID)[:, rows, :],
                                            WtT[:, j, :], Xv[:, rows, :, j], start=(j == 0), stop=(j == PX - 1))
            last.then_inc(pre_fill, 1)
            pe.wait_ge(pre_evac, 6)
            for b in range(B):
                last = nc.tensor.transpose(O[0:NPATCH, b * D:(b + 1) * D], tokT[:, b * NPATCH:(b + 1) * NPATCH],
                                           ident[:, :])
            last.then_inc(pre_fill, 1)
            pe.wait_ge(ld_attn, 16 * 3)
            for h in range(H):
                last = nc.tensor.matmul(slots[2][:, h * D:(h + 1) * D], WvT[:, h * D:(h + 1) * D], WoS[:, h, :],
                                        start=True, stop=True)
            last.then_inc(pre_fill, 1)
            pe.wait_ge(normed, 1)
            for b in range(B):
                pe.wait_ge(pre_evac, 6 + b)
                for t in range(NX):
                    last = nc.tensor.transpose(slots[b % 2][:, t * P:(t + 1) * P], xn_all[:, b * NT + t, :], ident[:, :])
                last.then_inc(pre_fill, 1)
            pe.wait_ge(normed, 2)
            for b in range(B):
                last = nc.tensor.transpose(O[:, b * P:(b + 1) * P], xn_all[:, b * NT + NX, :], ident[:, :])
            last.then_inc(pre_fill, 1)
            pe.wait_ge(pre_evac, 7 + B)

            def turn_tile(row):
                pe.wait_ge(x3_done, row + 1)
                nc.tensor.transpose(PTf[:, NT * P:(NT + 1) * P], x3[:, :], ident[:, :]).then_inc(x3_turned, 1)

            def route_tile(row):
                pe.wait_ge(x3_evac, row + 1)
                nc.tensor.matmul(PTf[:, LG:LG + E], x3T[:, :], WsS[:, :], start=True, stop=True).then_inc(lg_done, 1)

            def rank_tile(row):
                pe.wait_ge(hot_ready, row + 1)
                nc.tensor.matmul(PTf[:, RK:RK + E], before_r[:, :], hot[:, :], start=True, stop=True)
                nc.tensor.matmul(PTf[:, RK + E:RK + 2 * E], ones_r[:, :], hot[:, :], start=True, stop=True)\
                    .then_inc(ranks_done, 1)

            with pe.Fori(0, B) as b:
                at_step = pe.snap(b * STEPS)
                at_tile = pe.snap(b * NT)
                at_slot = [pe.snap(b * n) for n in PER_SLOT]

                def slot_for(*fill):
                    _, slot, k = FILL[fill]
                    pe.wait_ge(free[slot], at_slot[slot] + (k + 1))
                    return slots[slot]

                def queries(t):
                    pe.wait_ge(q_lo, (at_tile + t) * 2 + 1)
                    for i in range(H // 2):
                        last = nc.tensor.matmul(Q[:, i * P:(i + 1) * P], WqS[:, i * P:(i + 1) * P],
                                                xs[:, t * P:(t + 1) * P], start=True, stop=True)
                    last.then_inc(q_psum, 1)

                def scores(g):
                    t, h = divmod(g, H)
                    to = slot_for("scores", g)
                    if h == 0:
                        pe.wait_ge(q_crossed_hi, (at_tile + t) * 2 + 2)
                        pe.wait_ge(q_crossed_lo, (at_tile + t) * 2 + 2)
                    for a, c in ((0, FIRST), (FIRST, SP)):
                        for part, query in enumerate((QS, QX)):
                            last = nc.tensor.matmul(to[:, AT + a:AT + c], query[:, t % 2, h, :], KHL[:, h, a:c],
                                                    start=(part == 0), stop=(part == 1))
                    last.then_inc(filled, 1)

                def turn(g):
                    pe.wait_ge(p_normed, at_step + (g + 1))
                    if g >= 1:
                        pe.wait_ge(pt_evac, at_step + g)
                    if g % H == 7:
                        turn_tile(at_tile + g // H)
                    if g % H == 1:
                        route_tile(at_tile + g // H)
                    if g % H == 5:
                        rank_tile(at_tile + g // H)
                    for t in range(NT):
                        n = P if t < NX else TAIL
                        last = nc.tensor.transpose(PTf[0:n, t * P:(t + 1) * P], pn[:, g % 2, t * P:t * P + n], ident[:, :])
                    last.then_inc(p_turned, 1)

                def values(g):
                    tile, h = divmod(g, H)
                    pe.wait_ge(pt_evac, at_step + (g + 1))
                    if h == 0:
                        pe.wait_ge(y_done, at_tile + (tile + 1))
                    for t in range(NT):
                        n = P if t < NX else TAIL
                        last = nc.tensor.matmul(O[:, 0:D], pT[0:n, g % 2, t * P:(t + 1) * P],
                                                Vt[0:n, t, h * D:(h + 1) * D],
                                                start=(h == 0 and t == 0), stop=(h == H - 1 and t == NX))
                    last.then_inc(pv_done, 1)

                pe.wait_ge(xs_ready, b + 1)
                for pair in range(H // 2):
                    to = slot_for("keys", pair)
                    for a, c in ((0, FIRST), (FIRST, SP)):
                        last = nc.tensor.matmul(to[:, AT + a:AT + c], WkS[:, pair * P:(pair + 1) * P], xs[:, a:c],
                                                start=True, stop=True)
                    last.then_inc(filled, 1)
                queries(0)
                for kind, t in fills[H // 2:H // 2 + NT + LEAD]:
                    if kind == "scores":
                        scores(t)
                        continue
                    to = slot_for("values", t)
                    for c in range(2):
                        last = nc.tensor.matmul(to[:, c * 512:(c + 1) * 512], xs[:, t * P:(t + 1) * P],
                                                VO[:, c * 512:(c + 1) * 512], start=True, stop=True)
                    last.then_inc(filled, 1)
                for g in range(STEPS):
                    if g % H == QSTEP and g // H + 1 < NT:
                        queries(g // H + 1)
                    if g + LEAD < STEPS:
                        scores(g + LEAD)
                    if g >= 1:
                        turn(g - 1)
                    if g >= 2:
                        values(g - 2)
                turn(STEPS - 1)
                values(STEPS - 2)
                values(STEPS - 1)

            pe.wait_ge(ld_experts, 16 * 4)
            nc.tensor.transpose(Q[:, 0:E * NF], b1S, ident[0:E * NF, 0:E * NF]).then_inc(b1_turned, 1)
            pe.wait_ge(pt_evac, B * STEPS)
            route_tile(TILES)
            rank_tile(TILES)
            pe.wait_ge(ranks_evac, TILES + 1)
            turn_tile(TILES)
            route_tile(TILES + 1)
            rank_tile(TILES + 1)

            pe.wait_ge(experts_ready, 1)
            pe.wait_ge(counted, TILES + 3)
            pe.wait_ge(ld_experts, 16 * 4)

            def expert(i):
                return pe.value_load(exi[0:1, bass.ds(i, 1)], min_val=0, max_val=E - 1)

            def turn_rows(i, s):
                pe.wait_ge(xf_ready, i + 1)
                nc.tensor.transpose(Q[:, 0:P], xf[:, s, :], ident[:, :]).then_inc(f_turned, 1)

            def up(i, s):
                pe.wait_ge(w1_ready, i + 1)
                pe.wait_ge(fT_ready, i + 1)
                for c in range(NF):
                    last = nc.tensor.matmul(SL[:, s, c * P:(c + 1) * P], w1[:, s, c * P:(c + 1) * P], fT[:, s, :],
                                            start=True, stop=True)
                last.then_inc(up_done, 1)

            def down(i, s):
                e = expert(i)
                pe.wait_ge(gelu_done, i + 1)
                if not isinstance(i, int) or i > 0:
                    pe.wait_ge(yb_done, i * 2)
                for c in range(NF):
                    last = nc.tensor.matmul(O[:, 0:D], hidT[:, s, c * P:(c + 1) * P],
                                            W2S[:, bass.ds(e * (NF * D) + c * D, D)],
                                            start=(c == 0), stop=(c == NF - 1))
                last.then_inc(down_done, 1)

            turn_rows(0, 0)
            up(0, 0)
            turn_rows(1, 1)
            up(1, 1)
            turn_rows(2, 2)
            for i, s, _ in expert_tiles(pe):
                if later(i, 3):
                    pe.wait_ge(fT_ready, i + 3)
                    turn_rows(i + 3, (s + 3) % UN)
                if later(i, 2):
                    up(i + 2, (s + 2) % UN)
                down(i, s)


LEAD, QSTEP = 3, 0
QSTEPS_ACT, QSTEPS_VEC = (0, 2), (1, 3)
POW2, POW3 = 4, 6

_INS = ['x', 'txt', 'L0_tok_W', 'L0_tok_b', 'L0_tok_class_token', 'L0_tok_pos_embed', 'L0_attn_Wq', 'L0_attn_Wk',
        'L0_attn_Wv', 'L0_attn_Wo', 'L0_attn_bo', 'L0_attn_gamma', 'L0_attn_beta', 'L0_ffn_Ws', 'L0_ffn_bs',
        'L0_ffn_W1', 'L0_ffn_b1', 'L0_ffn_W2', 'L0_ffn_b2']


def kernel(**inputs):
    import numpy as _np
    import concourse.bacc as _bacc
    from concourse import mybir as _mybir
    from concourse.bass_utils import run_bass_kernel_spmd as _run

    nc = _bacc.Bacc("TRN2", target_bir_lowering=False, num_devices=1)
    arrays, args = {}, []
    for name in _INS:
        a = _np.ascontiguousarray(inputs[name])
        arrays[f"in_{name}_dram"] = a
        args.append(nc.dram_tensor(f"in_{name}_dram", a.shape, _mybir.dt.from_np(a.dtype), kind="ExternalInput").ap())
    B, C, IMG, _ = inputs['x'].shape
    NTXT, D = inputs['txt'].shape[1:]
    S = inputs['L0_tok_pos_embed'].shape[0] + NTXT
    E = inputs['L0_ffn_Ws'].shape[1]
    out = nc.dram_tensor("out_0_dram", (B, S, D), _mybir.dt.float32, kind="ExternalOutput").ap()
    tiles = -(-B * S // 128)
    n_rows = (E * tiles + -(-S // 128)) * 128
    by_expert = nc.dram_tensor("rows_by_expert", (n_rows, D + 4), _mybir.dt.float32, kind="Internal").ap()
    early_fusion_kernel(nc, *args, out, by_expert)
    r = _run(nc, [arrays], core_ids=[0])
    return r.results[0]["out_0_dram"]
```
